# Optimizing a Trainium2 kernel written in Bass

```python
import numpy as np
import jax
import jax.numpy as jnp

def _softmax(x, axis=-1):
    return jax.nn.softmax(x, axis=axis)

def _gelu(x):
    return jax.nn.gelu(x, approximate=True)

def _silu(x):
    return jax.nn.silu(x)

def _sigmoid(x):
    return jax.nn.sigmoid(x)

def _layernorm(x, axis=-1, eps=1e-05):
    m = jnp.mean(x, axis=axis, keepdims=True)
    v = jnp.var(x, axis=axis, keepdims=True)
    return (x - m) / jnp.sqrt(v + eps)

def _scatter_add(tgt, idx, src, axis=0):
    return tgt.at[idx].add(src)

def _segment_sum(src, seg, n):
    return jax.ops.segment_sum(src, seg, n)
kernel_name = 'mk_recurrent_d1_jaxref_r4_cca3bb'

def setup_inputs(seed: int=0):
    np.random.seed(seed)
    _w = jnp.asarray

    def _L0_attn_setup():
        import jax, jax.numpy as jnp
        import numpy as np
        BATCH, SEQ, D_MODEL, N_HEADS, D_HEAD = (2, 512, 512, 16, 128)
        ATTN_SCALE = np.sqrt(D_HEAD).astype(np.float32)
        IGNORE = jnp.float32(-100000.0)
        key = jax.random.key(seed)
        ks = jax.random.split(key, 5)
        init = 1.0 / np.sqrt(D_MODEL)
        return {'x': jax.random.normal(ks[0], (BATCH, SEQ, D_MODEL), jnp.float32), 'W_Q': jax.random.normal(ks[1], (N_HEADS, D_MODEL, D_HEAD), jnp.float32) * init, 'W_K': jax.random.normal(ks[2], (N_HEADS, D_MODEL, D_HEAD), jnp.float32) * init, 'W_V': jax.random.normal(ks[3], (N_HEADS, D_MODEL, D_HEAD), jnp.float32) * init, 'W_O': jax.random.normal(ks[4], (N_HEADS, D_HEAD, D_MODEL), jnp.float32) * init, 'b_Q': jnp.zeros((N_HEADS, D_HEAD), jnp.float32), 'b_K': jnp.zeros((N_HEADS, D_HEAD), jnp.float32), 'b_V': jnp.zeros((N_HEADS, D_HEAD), jnp.float32), 'b_O': jnp.zeros((D_MODEL,), jnp.float32)}
    _L0_attn_in = _L0_attn_setup()

    def _L0_ffn_setup():
        import jax, jax.numpy as jnp
        import numpy as np
        HIDDEN = 512
        INTER = 1408
        B, S = (2, 512)

        def _ternary(key, shape):
            return jax.random.randint(key, shape, -1, 2).astype(jnp.float32)
        key = jax.random.key(seed)
        ks = jax.random.split(key, 7)
        x = jax.random.normal(ks[0], (B, S, HIDDEN), dtype=jnp.float32)
        gate_w = _ternary(ks[1], (INTER, HIDDEN))
        up_w = _ternary(ks[2], (INTER, HIDDEN))
        down_w = _ternary(ks[3], (HIDDEN, INTER))
        gate_s = jax.random.uniform(ks[4], (INTER,), minval=0.01, maxval=0.1, dtype=jnp.float32)
        up_s = jax.random.uniform(ks[5], (INTER,), minval=0.01, maxval=0.1, dtype=jnp.float32)
        down_s = jax.random.uniform(ks[6], (HIDDEN,), minval=0.01, maxval=0.1, dtype=jnp.float32)
        return {'x': x, 'gate_w': gate_w, 'up_w': up_w, 'down_w': down_w, 'gate_s': gate_s, 'up_s': up_s, 'down_s': down_s}
    _L0_ffn_in = _L0_ffn_setup()
    _d = {'L0_attn_x': _L0_attn_in['x'], 'L0_attn_W_Q': _L0_attn_in['W_Q'], 'L0_attn_W_K': _L0_attn_in['W_K'], 'L0_attn_W_V': _L0_attn_in['W_V'], 'L0_attn_W_O': _L0_attn_in['W_O'], 'L0_attn_b_Q': _L0_attn_in['b_Q'], 'L0_attn_b_K': _L0_attn_in['b_K'], 'L0_attn_b_V': _L0_attn_in['b_V'], 'L0_attn_b_O': _L0_attn_in['b_O'], 'L0_ffn_gate_w': _L0_ffn_in['gate_w'], 'L0_ffn_up_w': _L0_ffn_in['up_w'], 'L0_ffn_down_w': _L0_ffn_in['down_w'], 'L0_ffn_gate_s': _L0_ffn_in['gate_s'], 'L0_ffn_up_s': _L0_ffn_in['up_s'], 'L0_ffn_down_s': _L0_ffn_in['down_s']}
    _x0 = _d['L0_attn_x']
    _d['L0_attn_x'] = jax.random.normal(jax.random.fold_in(jax.random.key(seed), 1), (4, 512, 512), dtype=_x0.dtype)
    del _x0
    return _d

def reference(L0_attn_x, L0_attn_W_Q, L0_attn_W_K, L0_attn_W_V, L0_attn_W_O, L0_attn_b_Q, L0_attn_b_K, L0_attn_b_V, L0_attn_b_O, L0_ffn_gate_w, L0_ffn_up_w, L0_ffn_down_w, L0_ffn_gate_s, L0_ffn_up_s, L0_ffn_down_s):

    def _L0_attn_ref(x, W_Q, W_K, W_V, W_O, b_Q, b_K, b_V, b_O):
        import jax, jax.numpy as jnp
        import numpy as np
        BATCH, SEQ, D_MODEL, N_HEADS, D_HEAD = (2, 512, 512, 16, 128)
        ATTN_SCALE = np.sqrt(D_HEAD).astype(np.float32)
        IGNORE = jnp.float32(-100000.0)
        q = jnp.einsum('bpd,hde->bphe', x, W_Q) + b_Q
        k = jnp.einsum('bpd,hde->bphe', x, W_K) + b_K
        v = jnp.einsum('bpd,hde->bphe', x, W_V) + b_V
        scores = jnp.einsum('bqhe,bkhe->bhqk', q, k) / ATTN_SCALE
        S = x.shape[1]
        causal = jnp.tril(jnp.ones((S, S), bool))
        scores = jnp.where(causal, scores, IGNORE)
        attn = jax.nn.softmax(scores, axis=-1)
        z = jnp.einsum('bkhe,bhqk->bqhe', v, attn)
        out = jnp.einsum('bqhe,hed->bqd', z, W_O) + b_O
        return out

    def _L0_ffn_ref(x, gate_w, up_w, down_w, gate_s, up_s, down_s):
        import jax, jax.numpy as jnp
        import numpy as np
        HIDDEN = 512
        INTER = 1408
        B, S = (2, 512)

        def _ternary(key, shape):
            return jax.random.randint(key, shape, -1, 2).astype(jnp.float32)
        b, s, h = x.shape
        xf = x.reshape(b * s, h)
        g = jnp.einsum('th,ih->ti', xf, gate_w) * gate_s
        u = jnp.einsum('th,ih->ti', xf, up_w) * up_s
        hdn = jax.nn.silu(g) * u
        out = jnp.einsum('ti,hi->th', hdn, down_w) * down_s
        return out.reshape(b, s, -1)
    x = L0_attn_x
    xn = _layernorm(x, axis=-1)
    s = _L0_attn_ref(xn, L0_attn_W_Q, L0_attn_W_K, L0_attn_W_V, L0_attn_W_O, L0_attn_b_Q, L0_attn_b_K, L0_attn_b_V, L0_attn_b_O)
    g = _silu(_L0_ffn_ref(xn, L0_ffn_gate_w, L0_ffn_up_w, L0_ffn_down_w, L0_ffn_gate_s, L0_ffn_up_s, L0_ffn_down_s))
    x = x + s * g
    return x

_drawn_inputs = setup_inputs


def setup_inputs(seed=0):
    import zlib

    import numpy as np

    out = dict(_drawn_inputs(seed))
    spreads = {'L0_attn_b_Q': (0.0, 0.315),
     'L0_attn_b_K': (0.0, 0.8),
     'L0_attn_b_V': (0.0, 0.1),
     'L0_attn_b_O': (0.0, 0.1)}
    factors = {}
    for name, (base, spread) in spreads.items():
        noise = np.random.default_rng([zlib.crc32(name.encode()), seed]).standard_normal(out[name].shape)
        drawn = base * np.exp(spread * noise) if base else spread * noise
        out[name] = jnp.asarray(drawn.astype(out[name].dtype))
    for name, factor in factors.items():
        out[name] = (out[name] * factor).astype(out[name].dtype)
    return out
```

```python
from contextlib import ExitStack

import concourse.bass as bass
from concourse import mybir

ALU = mybir.AluOpType
ACT = mybir.ActivationFunctionType
AX_X = mybir.AxisListType.X
F32 = mybir.dt.float32
F16 = mybir.dt.float16
ds = bass.ds

P = 128
B, S, D = 4, 512, 512
T = B * S
H, E = 16, 128
F = 1408
KT = D // P
TT = S // P
MT = F // P
HG = 4
NU = B * H
SLICES = 4 * KT
V_SL, Q_SL, K_SL, O_SL = 0, KT, 2 * KT, 3 * KT
WS = 16.0
SCORE_SCALE = float(E) ** -0.5 / WS ** 2
MASKED = -1.0e5 / SCORE_SCALE
EPS = 1e-5

SCORE_TILES = [(3, 0, 0, 0), (2, 1, 0, 512), (0, 1, 384, 896), (1, 2, 0, 1024)]
P_AT = {i: at for i, _, _, at in SCORE_TILES}
DIAGONALS = [(0, 384, 1), (1, 256, 2), (2, 128, 1)]
KEY_TILES = [(0, 0, 0, 0), (1, 1, 0, 512), (3, 1, 384, 896), (2, 2, 0, 1024)]
BANK_SPANS = [(0, 512), (512, 512), (1024, 256)]
PW = 1280

PASSES = ((0, 0), (0, 1), (1, 0))


def a0_before_q(u, more_v=True):
    return 3 + 2 * u if more_v else 63 + u


def a1_before_k(u, with_out=True):
    return 2 * u - 1 if with_out else 3 + u


def slot_of(m):
    return m % 2 if m < MT - 1 else 2


def build(nc, x, ffn_w, attn_w, cols, b_o, down_s, out):
    x_chunks = x.rearrange("(c t p) d -> c p t d", t=TT, p=P)
    x_tiles = x.rearrange("(t p) d -> t p d", p=P)
    out_tiles = out.rearrange("(t p) d -> t p d", p=P)
    parked = nc.dram_tensor("parked_silu", (T, D), F32, kind="Internal").ap()
    parked_chunks = parked.rearrange("(c t p) d -> c p t d", t=TT, p=P)
    parked_tiles = parked.rearrange("(t p) d -> t p d", p=P)

    with ExitStack() as ctx:
        def sb(name, shape, dt):
            return ctx.enter_context(nc.sbuf_tensor(name, shape, dt))

        def sem(name):
            return ctx.enter_context(nc.semaphore(name))

        group = 2 * SLICES * 512
        arena = sb("arena", [P, 69632], F16)

        def carve(at, size, dt=F16):
            part = arena[:, at:at + size * (2 if dt == F32 else 1)]
            return (part.bitcast(F32) if dt == F32 else part), at + size * (2 if dt == F32 else 1)

        fw, at = carve(group, 2 * MT * 3 * 512)
        FW = [fw.rearrange("p (s m w n) -> p s m w n", s=2, m=MT, w=3)[:, part] for part in (0, 1)]
        x_in, at = carve(at, TT * D, F32)
        ffn_in, at = carve(at, 2 * 3 * 512, F32)
        silu_gate, at = carve(at, S, F32)
        hidden, at = carve(at, S, F32)
        ht, at = carve(at, 2 * 3 * S)
        ffn_out, at = carve(at, TT * D, F32)
        x_in = x_in.rearrange("p (t d) -> p t d", t=TT)
        ffn_in = ffn_in.rearrange("p (s w n) -> p s w n", s=2, w=3)
        HT = [ht.rearrange("p (a s n) -> p a s n", a=2, s=3)[:, part] for part in (0, 1)]
        ffn_out = ffn_out.rearrange("p (t d) -> p t d", t=TT)
        W, at = carve(0, 2 * group)
        z, at = carve(at, 2 * 2 * HG * S)
        pt, at = carve(at, 2 * PW)
        probs, at = carve(at, PW, F32)
        acc, at = carve(at, (T // P) * D, F32)
        x_again, at = carve(at, 2 * D, F32)
        silu_again, at = carve(at, 2 * D, F32)
        Z = [z.rearrange("p (s b h n) -> p s b h n", s=2, b=2, h=HG)[:, part] for part in (0, 1)]
        PT = [pt.rearrange("p (s n) -> p s n", s=2)[:, part] for part in (0, 1)]
        acc = acc.rearrange("p (t d) -> p t d", d=D)
        x_again = x_again.rearrange("p (s d) -> p s d", s=2)
        silu_again = silu_again.rearrange("p (s d) -> p s d", s=2)

        XT = [sb(f"XT_{n}", [P, KT, T], F16) for n in ("hi", "lo")]
        V = [sb(f"V_{n}", [P, 2, TT, HG * E], F16) for n in ("hi", "lo")]
        Q = [sb(f"Q_{n}", [P, S], F16) for n in ("hi", "lo")]
        K = [sb(f"K_{n}", [P, S], F16) for n in ("hi", "lo")]
        w_in = sb("w_in", [P, 2, 512], F32)
        ident = sb("ident", [P, P], F32)
        mask = sb("mask", [P, 2, P], F32)
        cols_in = sb("cols_in", [P, 3 * H + 2 * MT], F32)
        biases = sb("biases", [P, 3 * H], F32)
        ffn_scales = sb("ffn_scales", [P, 2 * MT], F32)
        b_o_rows = sb("b_o_rows", [P, D], F32)
        down_rows = sb("down_rows", [P, D], F32)
        stats = sb("stats", [P, TT, 6], F32)
        moments = sb("moments", [P, TT, 2], F32)
        var_eps = sb("var_eps", [P, TT], F32)
        std = sb("std", [P, TT], F32)
        rstd0 = sb("rstd0", [P, TT], F32)
        newton_a = sb("newton_a", [P, TT], F32)
        newton_b = sb("newton_b", [P, TT], F32)
        rstd = sb("rstd", [P, TT], F32)
        row_max = sb("row_max", [P, TT], F32)
        neg_max = sb("neg_max", [P, TT], F32)
        row_sum = sb("row_sum", [P, TT], F32)
        inv_sum = sb("inv_sum", [P, TT], F32)

        bank = [ctx.enter_context(nc.psum_tensor(f"bank{i}", [P, 512], F32)) for i in range(8)]
        GATE, UP, XB, DOWN = bank[0], bank[1], bank[2:4], bank[4:8]
        A0, A1, SC, TR = bank[2], bank[3], [bank[0], bank[1], bank[4]], bank[5:8]
        ZB = TR[0]

        const_loaded = sem("const_loaded")
        const_scaled = sem("const_scaled")
        blank_ok = sem("blank_ok")
        ident_ok = sem("ident_ok")
        x_loaded = sem("x_loaded")
        stats_ok = sem("stats_ok")
        moments_ok = sem("moments_ok")
        var_ok = sem("var_ok")
        std_ok = sem("std_ok")
        rstd_step = sem("rstd_step")
        xn_ok = sem("xn_ok")
        xt_mm = sem("xt_mm")
        xt_hi = sem("xt_hi")
        xt_lo = sem("xt_lo")
        ffn_loaded = [sem("ffn_loaded0"), sem("ffn_loaded1")]
        fw_hi = sem("fw_hi")
        fw_lo = sem("fw_lo")
        gate_mm = sem("gate_mm")
        up_mm = sem("up_mm")
        gate_silu = sem("gate_silu")
        hidden_ok = sem("hidden_ok")
        ht_hi = sem("ht_hi")
        ht_lo = sem("ht_lo")
        down_mm = sem("down_mm")
        down_scaled = sem("down_scaled")
        down_silu = sem("down_silu")
        park_done = sem("park_done")
        w_loaded = sem("w_loaded")
        w_hi = sem("w_hi")
        w_lo = sem("w_lo")
        a0_mm = sem("a0_mm")
        a1_mm = sem("a1_mm")
        a0_hi = sem("a0_hi")
        a1_hi = sem("a1_hi")
        a0_lo = sem("a0_lo")
        a1_lo = sem("a1_lo")
        score_mm = sem("score_mm")
        masked = sem("masked")
        maxed = sem("maxed")
        negated = sem("negated")
        exp_ok = sem("exp_ok")
        inverted = sem("inverted")
        probs_ok = sem("probs_ok")
        t_mm = sem("t_mm")
        t_hi = sem("t_hi")
        t_lo = sem("t_lo")
        z_mm = sem("z_mm")
        z_hi = sem("z_hi")
        z_lo = sem("z_lo")
        acc_ready = sem("acc_ready")
        tail_loaded = [sem("tail_loaded0"), sem("tail_loaded1")]
        tail_mul = sem("tail_mul")
        tail_add = sem("tail_add")
        stored = [sem("stored0"), sem("stored1")]

        def w_at(owner, part, sl, col=0, width=512):
            at = ((owner // SLICES) % 2) * group + (part * SLICES * 512 + sl * 512 + col)
            return W[:, ds(at, width)]

        def head_of(u):
            return (u // SLICES) * HG + u % HG

        def bias_of(kind, u):
            return biases[:, ds(head_of(u) + kind * H, 1)]

        block = ctx.enter_context(nc.Block())

        @block.sync
        def _(sp):
            sp.dma_start(x_in, x_chunks[0]).then_inc(x_loaded, 16)
            for m in range(2):
                sp.dma_start(ffn_in[:, m], ffn_w[m]).then_inc(ffn_loaded[m], 16)
            sp.dma_start(cols_in[:], cols).then_inc(const_loaded, 16)
            sp.dma_start(down_rows[:], down_s.partition_broadcast(P)).then_inc(const_loaded, 16)
            sp.dma_start(b_o_rows[:], b_o.partition_broadcast(P)).then_inc(const_loaded, 16)
            sp.wait_ge(xt_mm, KT)
            sp.dma_start(x_in, x_chunks[1]).then_inc(x_loaded, 16)
            with sp.Fori(1, MT // 2) as i:
                for par in range(2):
                    sp.wait_ge(fw_lo, 3 * (2 * i + par - 1))
                    sp.dma_start(ffn_in[:, par], ffn_w[2 * i + par]).then_inc(ffn_loaded[par], 16)
            sp.wait_ge(fw_lo, 3 * (MT - 2))
            sp.dma_start(ffn_in[:, 0], ffn_w[MT - 1]).then_inc(ffn_loaded[0], 16)
            for c in range(2, B):
                sp.wait_ge(xt_mm, KT * c)
                sp.dma_start(x_in, x_chunks[c]).then_inc(x_loaded, 16)
            sp.dma_start(w_in[:, 0], attn_w[0]).then_inc(w_loaded, 16)
            with sp.Fori(1, B * SLICES) as sl:
                sp.wait_ge(w_lo, sl)
                sp.dma_start(w_in[:, sl % 2], attn_w[sl]).then_inc(w_loaded, 16)
            sp.wait_ge(park_done, 16 * B)
            for par in range(2):
                sp.dma_start(x_again[:, par], x_tiles[par]).then_inc(tail_loaded[par], 16)
                sp.dma_start(silu_again[:, par], parked_tiles[par]).then_inc(tail_loaded[par], 16)
            with sp.Fori(0, T // P // 2 - 1) as i:
                for par in range(2):
                    sp.wait_ge(tail_add, 2 * i + par + 1)
                    sp.dma_start(out_tiles[2 * i + par], silu_again[:, par]).then_inc(stored[par], 16)
                    sp.wait_ge(stored[par], 16 * (i + 1))
                    sp.dma_start(x_again[:, par], x_tiles[2 * i + par + 2]).then_inc(tail_loaded[par], 16)
                    sp.dma_start(silu_again[:, par], parked_tiles[2 * i + par + 2]).then_inc(tail_loaded[par], 16)
            for par in range(2):
                sp.wait_ge(tail_add, T // P - 1 + par)
                sp.dma_start(out_tiles[T // P - 2 + par], silu_again[:, par]).then_inc(stored[par], 16)
            for par in range(2):
                sp.wait_ge(stored[par], 16 * (T // P // 2))

        @block.gpsimd
        def _(pool):
            nc.gpsimd.memset(ident[:], 0.0).then_inc(blank_ok, 1)
            nc.gpsimd.memset(mask[:], 0.0).then_inc(blank_ok, 1)
            pool.wait_ge(blank_ok, 2)
            nc.gpsimd.affine_select(out=ident[:], in_=ident[:], compare_op=ALU.not_equal, fill=1.0, base=0,
                                    pattern=[[-1, P]], channel_multiplier=1).then_inc(ident_ok, 1)
            nc.gpsimd.affine_select(out=mask[:], in_=mask[:], compare_op=ALU.is_ge, fill=MASKED, base=0,
                                    pattern=[[0, 2], [-1, P]], channel_multiplier=1).then_inc(ident_ok, 1)
            pool.wait_ge(const_loaded, 48)
            nc.gpsimd.tensor_scalar(ffn_scales[:], cols_in[:, 3 * H:], 1.0 / WS, None, ALU.mult).then_inc(const_scaled, 1)
            nc.gpsimd.tensor_scalar(biases[:], cols_in[:, 0:3 * H], WS, None, ALU.mult).then_inc(const_scaled, 1)
            nc.gpsimd.tensor_scalar(down_rows[:], down_rows[:], 1.0 / WS, None, ALU.mult).then_inc(const_scaled, 1)
            pool.wait_ge(score_mm, 1)
            pool.wait_ge(park_done, 16 * B)
            with pool.Fori(0, T // P) as t:
                nc.gpsimd.tensor_copy(acc[:, t], b_o_rows[:]).then_inc(acc_ready, 1)

            def finish(t, par, turns, added):
                pool.wait_ge(tail_loaded[par], 32 * turns)
                pool.wait_ge(a1_lo, added)
                nc.gpsimd.tensor_tensor(silu_again[:, par], acc[:, t], silu_again[:, par],
                                        ALU.mult).then_inc(tail_mul, 1)
                pool.wait_ge(tail_mul, t + 1)
                nc.gpsimd.tensor_tensor(silu_again[:, par], silu_again[:, par], x_again[:, par],
                                        ALU.add).then_inc(tail_add, 1)

            with pool.Fori(0, 5) as i:
                for par in range(2):
                    finish(2 * i + par, par, i + 1, a1_before_k(2 * i + par + 53))
            finish(10, 0, 6, a1_before_k(63))
            for t in range(11, 16):
                finish(t, t % 2, t // 2 + 1, a1_before_k(63) + t - 10)

        @block.tensor
        def _(pe):
            def product(out, stationary, moving, tiles, first=True, last=True):
                for n, k in enumerate(tiles):
                    for i, (a, b) in enumerate(PASSES):
                        mm = nc.tensor.matmul(out, stationary(a, k), moving(b, k),
                                              start=first and n == 0 and i == 0,
                                              stop=last and n == len(tiles) - 1 and i == 2)
                return mm

            def transpose_x(c, k):
                if k == 0:
                    pe.wait_ge(xn_ok, c + 1)
                if k >= 2:
                    pe.wait_ge(xt_lo, KT * c + k - 1)
                for t in range(TT):
                    tr = nc.tensor.transpose(XB[k % 2][:, t * P:(t + 1) * P], x_in[:, t, k * P:(k + 1) * P], ident[:])
                tr.then_inc(xt_mm, 1)

            def project_ffn(bank_, w, c, m):
                return product(bank_[:], lambda a, k: FW[a][:, m, w, k * P:(k + 1) * P],
                               lambda b, k: XT[b][:, k, ds(c * S, S)], range(KT))

            def down(c, m, slot, tiles, start, stop):
                for t in tiles:
                    if start and not (isinstance(c, int) and c == 0):
                        pe.wait_ge(down_scaled, TT * (c - 1) + t + 1)
                    mm = product(DOWN[t][:], lambda a, _: HT[a][:, slot, t * P:(t + 1) * P],
                                 lambda b, _: FW[b][:, m, 2, :], [0], start, stop)
                    if stop:
                        mm.then_inc(down_mm, 1)

            def step(c, m, slot, before=None, first_chunk=False):
                n = MT * c + m
                if first_chunk:
                    pe.wait_ge(fw_lo, 3 * m + 1)
                if isinstance(m, int) and m == 0:
                    pe.wait_ge(xt_lo, KT * (c + 1))
                if before:
                    pe.wait_ge(gate_silu, n)
                project_ffn(GATE, 0, c, m).then_inc(gate_mm, 1)
                if before:
                    first, final = (isinstance(before[1], int) and before[1] == v for v in (0, MT - 1))
                    if first_chunk:
                        pe.wait_ge(fw_lo, 3 * m)
                    pe.wait_ge(ht_lo, n)
                    down(*before, (0, 1), first, final)
                    pe.wait_ge(hidden_ok, n)
                if first_chunk:
                    pe.wait_ge(fw_lo, 3 * m + 2)
                project_ffn(UP, 1, c, m).then_inc(up_mm, 1)
                if before:
                    down(*before, (2, 3), first, final)

            def chunk(c, first_chunk=False, last_chunk=False):
                def steps(lo, hi):
                    with pe.Fori(lo // 2, hi // 2) as i:
                        for par in range(2):
                            step(c, 2 * i + par, par, (c, 2 * i + par - 1, 1 - par), first_chunk)

                step(c, 1, 1, (c, 0, 0), first_chunk)
                steps(2, 6)
                if not last_chunk:
                    transpose_x(c + 1, 0)
                    transpose_x(c + 1, 1)
                steps(6, 10)
                if not last_chunk:
                    transpose_x(c + 1, 2)
                    transpose_x(c + 1, 3)
                step(c, MT - 1, 2, (c, MT - 2, 1), first_chunk)
                if not last_chunk:
                    step(c + 1, 0, 0, (c, MT - 1, 2))

            pe.wait_ge(ident_ok, 1)
            for k in range(KT):
                transpose_x(0, k)
            step(0, 0, 0, None, True)
            chunk(0, first_chunk=True)
            with pe.Fori(1, B - 1) as c:
                chunk(c)
            chunk(B - 1, last_chunk=True)

            def project_head(bank_, sl, n, signal):
                xo = ((n // HG) % B) * S
                product(bank_[:], lambda a, k: w_at(n, a, sl + k, (n % HG) * E, E),
                        lambda b, k: XT[b][:, k, ds(xo, S)], range(KT)).then_inc(signal, 1)

            def project_v(bank_, t, signal):
                product(bank_[:], lambda a, k: XT[a][:, k, ds((t % (T // P)) * P, P)],
                        lambda b, k: w_at(t, b, V_SL + k), range(KT)).then_inc(signal, 1)

            def scores():
                for i, b_, col, _ in SCORE_TILES:
                    width = (i + 1) * P
                    mm = product(SC[b_][:, col:col + width], lambda a, _: Q[a][:, i * P:(i + 1) * P],
                                 lambda b, _: K[b][:, 0:width], [0])
                    if i != 2:
                        mm.then_inc(score_mm, 1)

            def transpose_probs(u):
                pe.wait_ge(probs_ok, u + 1)
                if not (isinstance(u, int) and u == 0):
                    pe.wait_ge(z_lo, u)
                for j, b_, col, _ in KEY_TILES:
                    for i in range(j, TT):
                        at = P_AT[i] + j * P
                        tr = nc.tensor.transpose(TR[b_][:, col + (i - j) * P:col + (i - j + 1) * P],
                                                 probs[:, at:at + P], ident[:])
                    if j != 1:
                        tr.then_inc(t_mm, 1)

            def weigh_v(u):
                for n, (j, b_, _, at) in enumerate(KEY_TILES):
                    pe.wait_ge(t_lo, 3 * u + b_ + 1)
                    mm = product(ZB[:, j * P:], lambda a, _: V[a][:, (u // HG) % 2, j, ds((u % HG) * E, E)],
                                 lambda b, _: PT[b][:, at:at + S - j * P], [0], n == 0, n == TT - 1)
                mm.then_inc(z_mm, 1)

            def project_out(t):
                product(A1[:], lambda a, j: Z[a][:, (t // TT) % 2, j, ds((t % TT) * P, P)],
                        lambda b, j: w_at(t, b, O_SL + j), range(HG)).then_inc(a1_mm, 1)

            def unit(u, ahead=True, more_v=True, more_w=True, with_out=True):
                if more_w:
                    pe.wait_ge(w_lo, u + 13)
                if ahead:
                    pe.wait_ge(a0_lo, a0_before_q(u, more_v))
                    project_head(A0, Q_SL, u + 1, a0_mm)
                    pe.wait_ge(a1_lo, a1_before_k(u, with_out))
                    project_head(A1, K_SL, u + 1, a1_mm)
                transpose_probs(u)
                if more_v:
                    pe.wait_ge(a0_lo, a0_before_q(u) + 1)
                    project_v(A0, u + 4, a0_mm)
                if ahead:
                    pe.wait_ge(a0_lo, a0_before_q(u, more_v) + 1)
                    pe.wait_ge(a1_lo, a1_before_k(u, with_out) + 1)
                    scores()
                if with_out:
                    if not ahead:
                        pe.wait_ge(a1_lo, a1_before_k(u))
                    project_out(u - 4)
                weigh_v(u)

            pe.wait_ge(w_lo, SLICES)
            project_head(A0, Q_SL, 0, a0_mm)
            project_head(A1, K_SL, 0, a1_mm)
            pe.wait_ge(a0_lo, 1)
            project_v(A0, 0, a0_mm)
            pe.wait_ge(ht_lo, MT * B)
            down(B - 1, MT - 1, 2, (0, 1), False, True)
            pe.wait_ge(a1_lo, 1)
            project_v(A1, 1, a1_mm)
            down(B - 1, MT - 1, 2, (2, 3), False, True)
            pe.wait_ge(a0_lo, 2)
            project_v(A0, 2, a0_mm)
            pe.wait_ge(down_scaled, TT * (B - 1) + 1)
            scores()
            pe.wait_ge(a1_lo, 2)
            project_v(A1, 3, a1_mm)
            pe.wait_ge(down_scaled, TT * B)
            unit(0, with_out=False)
            with pe.Fori(1, 4) as u:
                unit(u, with_out=False)
            with pe.Fori(4, 48) as u:
                unit(u)
            pe.wait_ge(w_lo, B * SLICES)
            with pe.Fori(48, 60) as u:
                unit(u, more_w=False)
            with pe.Fori(60, 63) as u:
                unit(u, more_v=False, more_w=False)
            unit(63, ahead=False, more_v=False, more_w=False)
            pe.wait_ge(z_lo, NU)
            for t in range(60, 64):
                pe.wait_ge(a1_lo, a1_before_k(63) + t - 59)
                project_out(t)

        @block.scalar
        def _(act):
            def split_ffn(m, par):
                act.wait_ge(ffn_loaded[par], 16 * (m // 2 + 1))
                for w in range(3):
                    nc.scalar.activation(FW[0][:, m, w, :], ffn_in[:, par, w], ACT.Copy, scale=WS).then_inc(fw_hi, 1)

            def split_attn(sl):
                act.wait_ge(w_loaded, 16 * (sl + 1))
                nc.scalar.activation(w_at(sl, 0, sl % SLICES), w_in[:, sl % 2], ACT.Copy, scale=WS).then_inc(w_hi, 1)

            def root(c):
                act.wait_ge(var_ok, c + 1)
                nc.scalar.activation(std[:], var_eps[:], ACT.Sqrt).then_inc(std_ok, 1)

            def split_x(c, k):
                act.wait_ge(xt_mm, KT * c + k + 1)
                nc.scalar.activation(XT[0][:, k, ds(c * S, S)], XB[k % 2][:], ACT.Copy).then_inc(xt_hi, 1)

            def silu_down(c, tiles):
                for t in tiles:
                    act.wait_ge(down_scaled, TT * c + t + 1)
                    nc.scalar.activation(ffn_out[:, t], ffn_out[:, t], ACT.Silu).then_inc(down_silu, 1)

            def park(c):
                act.wait_ge(down_silu, TT * (c + 1))
                act.dma_start(parked_chunks[c], ffn_out).then_inc(park_done, 16)

            def step(c, m, slot, first_chunk=False, down_of=None):
                n = MT * c + m
                act.wait_ge(gate_mm, n + 1)
                nc.scalar.activation(silu_gate, GATE[:], ACT.Silu, scale=ffn_scales[:, ds(m, 1)]).then_inc(gate_silu, 1)
                if down_of is not None:
                    silu_down(down_of, (0, 1))
                act.wait_ge(hidden_ok, n + 1)
                nc.scalar.activation(HT[0][:, slot], hidden, ACT.Copy).then_inc(ht_hi, 1)
                if down_of is not None:
                    silu_down(down_of, (2, 3))
                    park(down_of)

            def chunk(c, first_chunk=False, last_chunk=False):
                def steps(lo, hi):
                    with act.Fori(lo // 2, hi // 2) as i:
                        for par in range(2):
                            step(c, 2 * i + par, par)
                            if first_chunk:
                                split_ffn(2 * i + par + 2, par)
                            if last_chunk:
                                split_attn(4 * i + 2 * par - 4)
                                split_attn(4 * i + 2 * par - 3)

                step(c, 1, 1)
                if first_chunk:
                    split_ffn(3, 1)
                if not last_chunk:
                    root(c + 1)
                steps(2, 6)
                if not last_chunk:
                    split_x(c + 1, 0)
                    split_x(c + 1, 1)
                if first_chunk:
                    with act.Fori(3, 4) as i:
                        for par in range(2):
                            step(c, 2 * i + par, par)
                            split_ffn(2 * i + par + 2, par)
                    step(c, 8, 0)
                    split_ffn(MT - 1, 0)
                    step(c, 9, 1)
                else:
                    steps(6, 10)
                if not last_chunk:
                    split_x(c + 1, 2)
                    split_x(c + 1, 3)
                step(c, MT - 1, 2)
                if not last_chunk:
                    step(c + 1, 0, 0, down_of=c)

            root(0)
            split_ffn(0, 0)
            for k in range(KT):
                split_x(0, k)
            act.wait_ge(const_scaled, 3)
            split_ffn(1, 1)
            step(0, 0, 0)
            split_ffn(2, 0)
            chunk(0, first_chunk=True)
            with act.Fori(1, B - 1) as c:
                chunk(c)
            chunk(B - 1, last_chunk=True)

            def split_head(u, kind, n, bank_, to, mm, mm_count, hi):
                act.wait_ge(mm, mm_count)
                nc.scalar.activation(to[0][:], bank_[:], ACT.Identity, bias=bias_of(kind, n)).then_inc(hi, 1)

            def split_v(t, bank_, mm, mm_count, hi):
                act.wait_ge(mm, mm_count)
                nc.scalar.activation(V[0][:, (t // TT) % 2, t % TT, :], bank_[:], ACT.Copy).then_inc(hi, 1)

            def exps(n):
                act.wait_ge(negated, n + 1)
                for i, b_, col, at in SCORE_TILES:
                    width = (i + 1) * P
                    e = nc.scalar.activation(probs[:, at:at + width], SC[b_][:, col:col + width], ACT.Exp,
                                             bias=neg_max[:, i:i + 1], scale=SCORE_SCALE,
                                             accum_out=row_sum[:, i:i + 1])
                e.then_inc(exp_ok, 1)

            def split_probs(u):
                for b_, (at, width) in enumerate(BANK_SPANS):
                    act.wait_ge(t_mm, 3 * u + b_ + 1)
                    nc.scalar.activation(PT[0][:, at:at + width], TR[b_][:, 0:width], ACT.Copy).then_inc(t_hi, 1)

            def split_z(u):
                act.wait_ge(z_mm, u + 1)
                nc.scalar.activation(Z[0][:, (u // HG) % 2, u % HG, :], ZB[:], ACT.Identity,
                                     bias=bias_of(2, u)).then_inc(z_hi, 1)

            def unit(u, ahead=True, more_v=True, more_w=True, with_out=True):
                if ahead:
                    split_head(u, 0, u + 1, A0, Q, a0_mm, a0_before_q(u, more_v) + 1, a0_hi)
                    split_head(u, 1, u + 1, A1, K, a1_mm, a1_before_k(u, with_out) + 1, a1_hi)
                split_probs(u)
                if more_v:
                    split_v(u + 4, A0, a0_mm, a0_before_q(u) + 2, a0_hi)
                if more_w:
                    split_attn(u + SLICES)
                if ahead:
                    exps(u + 1)
                split_z(u)

            split_head(0, 0, 0, A0, Q, a0_mm, 1, a0_hi)
            split_head(0, 1, 0, A1, K, a1_mm, 1, a1_hi)
            split_v(0, A0, a0_mm, 2, a0_hi)
            silu_down(B - 1, (0, 1))
            split_v(1, A1, a1_mm, 2, a1_hi)
            silu_down(B - 1, (2, 3))
            park(B - 1)
            split_v(2, A0, a0_mm, 3, a0_hi)
            exps(0)
            split_v(3, A1, a1_mm, 3, a1_hi)
            with act.Fori(0, 4) as u:
                unit(u, with_out=False)
            with act.Fori(4, 48) as u:
                unit(u)
            with act.Fori(48, 60) as u:
                unit(u, more_w=False)
            with act.Fori(60, 63) as u:
                unit(u, more_v=False, more_w=False)
            unit(63, ahead=False, more_v=False, more_w=False)

        @block.vector
        def _(dve):
            def split_ffn(m, count):
                for w in range(3):
                    dve.wait_ge(fw_hi, 3 * count + w - 2)
                    nc.vector.scalar_tensor_tensor(out=FW[1][:, m, w, :], in0=ffn_in[:, m % 2, w], scalar=WS,
                                                   in1=FW[0][:, m, w, :], op0=ALU.mult,
                                                   op1=ALU.subtract).then_inc(fw_lo, 1)

            def split_attn(sl):
                dve.wait_ge(w_hi, sl + 1)
                nc.vector.scalar_tensor_tensor(out=w_at(sl, 1, sl % SLICES), in0=w_in[:, sl % 2], scalar=WS,
                                               in1=w_at(sl, 0, sl % SLICES), op0=ALU.mult,
                                               op1=ALU.subtract).then_inc(w_lo, 1)

            def normalise(c):
                dve.wait_ge(x_loaded, 16 * (c + 1))
                for t in range(TT):
                    nc.vector.bn_stats(out=stats[:, t], in_=x_in[:, t]).then_inc(stats_ok, 1)
                for t in range(TT):
                    dve.wait_ge(stats_ok, TT * c + t + 1)
                    nc.vector.bn_aggr(out=moments[:, t], in_=stats[:, t]).then_inc(moments_ok, 1)
                dve.wait_ge(moments_ok, TT * (c + 1))
                nc.vector.tensor_scalar(var_eps[:], moments[:, :, 1], EPS, None, ALU.add).then_inc(var_ok, 1)
                dve.wait_ge(std_ok, c + 1)
                nc.vector.reciprocal(rstd0[:], std[:]).then_inc(rstd_step, 1)
                dve.wait_ge(rstd_step, 4 * c + 1)
                nc.vector.tensor_tensor(newton_a[:], rstd0[:], rstd0[:], ALU.mult).then_inc(rstd_step, 1)
                dve.wait_ge(rstd_step, 4 * c + 2)
                nc.vector.scalar_tensor_tensor(out=newton_b[:], in0=newton_a[:], scalar=-0.5, in1=var_eps[:],
                                               op0=ALU.mult, op1=ALU.mult).then_inc(rstd_step, 1)
                dve.wait_ge(rstd_step, 4 * c + 3)
                nc.vector.scalar_tensor_tensor(out=rstd[:], in0=newton_b[:], scalar=1.5, in1=rstd0[:],
                                               op0=ALU.add, op1=ALU.mult).then_inc(rstd_step, 1)
                dve.wait_ge(rstd_step, 4 * c + 4)
                for t in range(TT):
                    n = nc.vector.tensor_scalar(x_in[:, t], x_in[:, t], moments[:, t, 0:1], rstd[:, t:t + 1],
                                                ALU.subtract, ALU.mult)
                n.then_inc(xn_ok, 1)

            def split_x(c, k):
                dve.wait_ge(xt_hi, KT * c + k + 1)
                nc.vector.tensor_tensor(XT[1][:, k, ds(c * S, S)], XB[k % 2][:], XT[0][:, k, ds(c * S, S)],
                                        ALU.subtract).then_inc(xt_lo, 1)

            def scale_down(c, tiles):
                for t in tiles:
                    dve.wait_ge(down_mm, TT * c + t + 1)
                    if t == 0 and not (isinstance(c, int) and c == 0):
                        dve.wait_ge(park_done, 16 * c)
                    nc.vector.tensor_tensor(ffn_out[:, t], DOWN[t][:], down_rows[:], ALU.mult).then_inc(down_scaled, 1)

            def step(c, m, slot, down_of=None):
                n = MT * c + m
                if down_of is not None:
                    scale_down(down_of, (0, 1))
                dve.wait_ge(gate_silu, n + 1)
                dve.wait_ge(up_mm, n + 1)
                nc.vector.scalar_tensor_tensor(out=hidden, in0=UP[:], scalar=ffn_scales[:, ds(MT + m, 1)],
                                               in1=silu_gate, op0=ALU.mult, op1=ALU.mult).then_inc(hidden_ok, 1)
                dve.wait_ge(ht_hi, n + 1)
                nc.vector.tensor_tensor(HT[1][:, slot], hidden, HT[0][:, slot], ALU.subtract).then_inc(ht_lo, 1)
                if down_of is not None:
                    scale_down(down_of, (2, 3))

            def chunk(c, first_chunk=False, last_chunk=False):
                def steps(lo, hi):
                    with dve.Fori(lo // 2, hi // 2) as i:
                        for par in range(2):
                            step(c, 2 * i + par, par)
                            if first_chunk:
                                split_ffn_at(i, par)
                            if last_chunk:
                                split_attn(4 * i + 2 * par - 4)
                                split_attn(4 * i + 2 * par - 3)

                def split_ffn_at(i, par):
                    for w in range(3):
                        dve.wait_ge(fw_hi, 3 * (2 * i + par + 2) + w + 1)
                        nc.vector.scalar_tensor_tensor(out=FW[1][:, 2 * i + par + 2, w, :], in0=ffn_in[:, par, w],
                                                       scalar=WS, in1=FW[0][:, 2 * i + par + 2, w, :],
                                                       op0=ALU.mult, op1=ALU.subtract).then_inc(fw_lo, 1)

                step(c, 1, 1)
                if first_chunk:
                    split_ffn(3, 4)
                if not last_chunk:
                    normalise(c + 1)
                steps(2, 6)
                if not last_chunk:
                    split_x(c + 1, 0)
                    split_x(c + 1, 1)
                if first_chunk:
                    with dve.Fori(3, 4) as i:
                        for par in range(2):
                            step(c, 2 * i + par, par)
                            split_ffn_at(i, par)
                    step(c, 8, 0)
                    split_ffn(MT - 1, MT)
                    step(c, 9, 1)
                else:
                    steps(6, 10)
                if not last_chunk:
                    split_x(c + 1, 2)
                    split_x(c + 1, 3)
                step(c, MT - 1, 2)
                if not last_chunk:
                    step(c + 1, 0, 0, down_of=c)

            normalise(0)
            split_ffn(0, 1)
            for k in range(KT):
                split_x(0, k)
            dve.wait_ge(const_scaled, 3)
            split_ffn(1, 2)
            step(0, 0, 0)
            split_ffn(2, 3)
            chunk(0, first_chunk=True)
            for c in range(1, B - 1):
                chunk(c)
            chunk(B - 1, last_chunk=True)

            def split_head(kind, n, bank_, to, hi, hi_count, lo):
                dve.wait_ge(hi, hi_count)
                nc.vector.scalar_tensor_tensor(out=to[1][:], in0=bank_[:], scalar=bias_of(kind, n), in1=to[0][:],
                                               op0=ALU.add, op1=ALU.subtract).then_inc(lo, 1)

            def split_v(t, bank_, hi, hi_count, lo):
                dve.wait_ge(hi, hi_count)
                at = (t // TT) % 2
                nc.vector.tensor_tensor(V[1][:, at, t % TT, :], bank_[:], V[0][:, at, t % TT, :],
                                        ALU.subtract).then_inc(lo, 1)

            def maxima(n):
                for b_, col, blocks in DIAGONALS:
                    dve.wait_ge(score_mm, 3 * n + b_ + 1)
                    nc.vector.tensor_tensor(SC[b_][:, col:col + blocks * P], SC[b_][:, col:col + blocks * P],
                                            mask[:, 0:blocks, :].rearrange("p b k -> p (b k)"),
                                            ALU.add).then_inc(masked, 1)
                dve.wait_ge(masked, 3 * n + 3)
                for i, b_, col, _ in SCORE_TILES:
                    r = nc.vector.reduce_max(row_max[:, i:i + 1], SC[b_][:, col:col + (i + 1) * P], AX_X)
                r.then_inc(maxed, 1)
                dve.wait_ge(maxed, n + 1)
                nc.vector.tensor_scalar(neg_max[:], row_max[:], -SCORE_SCALE, None, ALU.mult).then_inc(negated, 1)

            def normalise_probs(n):
                dve.wait_ge(exp_ok, n + 1)
                nc.vector.reciprocal(inv_sum[:], row_sum[:]).then_inc(inverted, 1)
                dve.wait_ge(inverted, n + 1)
                for i, _, _, at in SCORE_TILES:
                    r = nc.vector.tensor_scalar(probs[:, at:at + (i + 1) * P], probs[:, at:at + (i + 1) * P],
                                                inv_sum[:, i:i + 1], None, ALU.mult)
                r.then_inc(probs_ok, 1)

            def split_probs(u):
                for b_, (at, width) in enumerate(BANK_SPANS):
                    dve.wait_ge(t_hi, 3 * u + b_ + 1)
                    nc.vector.tensor_tensor(PT[1][:, at:at + width], TR[b_][:, 0:width], PT[0][:, at:at + width],
                                            ALU.subtract).then_inc(t_lo, 1)

            def split_z(u):
                dve.wait_ge(z_hi, u + 1)
                at = (u // HG) % 2
                nc.vector.scalar_tensor_tensor(out=Z[1][:, at, u % HG, :], in0=ZB[:], scalar=bias_of(2, u),
                                               in1=Z[0][:, at, u % HG, :], op0=ALU.add,
                                               op1=ALU.subtract).then_inc(z_lo, 1)

            def add_out(t, mm_count):
                dve.wait_ge(a1_mm, mm_count)
                o = t % (T // P)
                nc.vector.scalar_tensor_tensor(out=acc[:, o], in0=A1[:], scalar=WS ** -2, in1=acc[:, o],
                                               op0=ALU.mult, op1=ALU.add).then_inc(a1_lo, 1)

            def unit(u, ahead=True, more_v=True, more_w=True, with_out=True):
                if ahead:
                    split_head(0, u + 1, A0, Q, a0_hi, a0_before_q(u, more_v) + 1, a0_lo)
                    split_head(1, u + 1, A1, K, a1_hi, 4 + u, a1_lo)
                split_probs(u)
                if more_v:
                    split_v(u + 4, A0, a0_hi, a0_before_q(u) + 2, a0_lo)
                if more_w:
                    split_attn(u + SLICES)
                if ahead:
                    maxima(u + 1)
                if with_out:
                    add_out(u - 4, a1_before_k(u) + (2 if ahead else 1))
                if ahead:
                    normalise_probs(u + 1)
                split_z(u)

            split_head(0, 0, A0, Q, a0_hi, 1, a0_lo)
            split_head(1, 0, A1, K, a1_hi, 1, a1_lo)
            split_v(0, A0, a0_hi, 2, a0_lo)
            scale_down(B - 1, (0, 1))
            split_v(1, A1, a1_hi, 2, a1_lo)
            scale_down(B - 1, (2, 3))
            split_v(2, A0, a0_hi, 3, a0_lo)
            dve.wait_ge(ident_ok, 2)
            maxima(0)
            split_v(3, A1, a1_hi, 3, a1_lo)
            normalise_probs(0)
            with dve.Fori(0, 4) as u:
                unit(u, with_out=False)
            dve.wait_ge(acc_ready, T // P)
            with dve.Fori(4, 48) as u:
                unit(u)
            with dve.Fori(48, 60) as u:
                unit(u, more_w=False)
            with dve.Fori(60, 63) as u:
                unit(u, more_v=False, more_w=False)
            unit(63, ahead=False, more_v=False, more_w=False)
            for t in range(60, 64):
                add_out(t, a1_before_k(63) + t - 58)


def kernel(L0_attn_x, L0_attn_W_Q, L0_attn_W_K, L0_attn_W_V, L0_attn_W_O, L0_attn_b_Q, L0_attn_b_K, L0_attn_b_V,
           L0_attn_b_O, L0_ffn_gate_w, L0_ffn_up_w, L0_ffn_down_w, L0_ffn_gate_s, L0_ffn_up_s, L0_ffn_down_s):
    import numpy as np
    import concourse.bacc as bacc
    from concourse.bass_utils import run_bass_kernel_spmd

    x = np.ascontiguousarray(L0_attn_x).reshape(T, D)

    def up_like(w):
        return np.asarray(w).reshape(MT, P, KT, P).transpose(0, 3, 2, 1).reshape(MT, P, 1, 512)
    down = np.asarray(L0_ffn_down_w).T.reshape(MT, P, 1, D)
    ffn_w = np.ascontiguousarray(np.concatenate([up_like(L0_ffn_gate_w), up_like(L0_ffn_up_w), down], axis=2))

    def by_feature(w):
        return np.asarray(w).reshape(H // HG, HG, KT, P, E).transpose(0, 2, 3, 1, 4).reshape(H // HG, KT, P, HG * E)
    w_o = np.asarray(L0_attn_W_O).reshape(H // HG, HG, E, D)
    attn_w = np.ascontiguousarray(np.concatenate(
        [by_feature(L0_attn_W_V), by_feature(L0_attn_W_Q), by_feature(L0_attn_W_K), w_o], axis=1)).reshape(-1, P, 512)

    cols = np.ascontiguousarray(np.concatenate(
        [np.asarray(b).T for b in (L0_attn_b_Q, L0_attn_b_K, L0_attn_b_V)]
        + [np.asarray(v).reshape(MT, P).T for v in (L0_ffn_gate_s, L0_ffn_up_s)], axis=1))

    arrays = {"x": x, "ffn_w": ffn_w, "attn_w": attn_w, "cols": cols,
              "b_o": np.ascontiguousarray(L0_attn_b_O), "down_s": np.ascontiguousarray(L0_ffn_down_s)}
    nc = bacc.Bacc("TRN2", target_bir_lowering=False, num_devices=1)
    args = [nc.dram_tensor(f"{n}_dram", a.shape, F32, kind="ExternalInput").ap() for n, a in arrays.items()]
    out = nc.dram_tensor("out_dram", (T, D), F32, kind="ExternalOutput").ap()
    build(nc, *args, out)
    r = run_bass_kernel_spmd(nc, [{f"{n}_dram": a for n, a in arrays.items()}], core_ids=[0])
    return r.results[0]["out_dram"].reshape(B, S, D)
```

```python
from contextlib import ExitStack

import concourse.bass as bass
from concourse import mybir

ALU = mybir.AluOpType
ACT = mybir.ActivationFunctionType
AX_X = mybir.AxisListType.X
F32 = mybir.dt.float32
F16 = mybir.dt.float16
ds = bass.ds

P = 128
B, S, D = 4, 512, 512
T = B * S
H, E = 16, 128
F = 1408
KT = D // P
TT = S // P
MT = F // P
HG = 4
NU = B * H
TAIL = T // P - TT
SLICES = 4 * KT
V_SL, Q_SL, K_SL, O_SL = 0, KT, 2 * KT, 3 * KT
WS = 16.0
SCORE_SCALE = float(E) ** -0.5 / WS ** 2
MASKED = -1.0e5 / SCORE_SCALE
EPS = 1e-5

SCORE_TILES = [(3, 0, 0, 0), (2, 1, 0, 512), (0, 1, 384, 896), (1, 2, 0, 1024)]
P_AT = {i: at for i, _, _, at in SCORE_TILES}
DIAGONALS = [(0, 384, 1), (1, 256, 2), (2, 128, 1)]
KEY_TILES = [(0, 0, 0, 0), (1, 1, 0, 512), (3, 1, 384, 896), (2, 2, 0, 1024)]
BANK_SPANS = [(0, 512), (512, 512), (1024, 256)]
PW = 1280

PASSES = ((0, 0), (0, 1), (1, 0))
EXACT_STATIONARY = ((0, 0), (0, 1))
EXACT_MOVING = ((0, 0), (1, 0))


def a0_before(u):
    return 3 + 2 * u


def a1_before(u, when):
    return {"early": 3 + u, "middle": 2 * u - 1, "late": 59 + u}[when]


def slot_of(m):
    return m % 2 if m < MT - 1 else 2


def build(nc, x, ffn_w, attn_w, cols, b_o, down_s, out):
    x_chunks = x.rearrange("(c t p) d -> c p t d", t=TT, p=P)
    x_tiles = x.rearrange("(t p) d -> t p d", p=P)
    out_tiles = out.rearrange("(t p) d -> t p d", p=P)
    parked = nc.dram_tensor("parked_silu", (T, D), F32, kind="Internal").ap()
    parked_chunks = parked.rearrange("(c t p) d -> c p t d", t=TT, p=P)
    parked_tiles = parked.rearrange("(t p) d -> t p d", p=P)

    with ExitStack() as ctx:
        def sb(name, shape, dt):
            return ctx.enter_context(nc.sbuf_tensor(name, shape, dt))

        def sem(name):
            return ctx.enter_context(nc.semaphore(name))

        group = 2 * SLICES * 512
        arena = sb("arena", [P, 69632], F16)

        def carve(at, size, dt=F16):
            part = arena[:, at:at + size * (2 if dt == F32 else 1)]
            return (part.bitcast(F32) if dt == F32 else part), at + size * (2 if dt == F32 else 1)

        fw, at = carve(group, 2 * MT * 3 * 512)
        FW = [fw.rearrange("p (s m w n) -> p s m w n", s=2, m=MT, w=3)[:, part] for part in (0, 1)]
        x_in, at = carve(at, TT * D, F32)
        ffn_in, at = carve(at, 2 * 3 * 512, F32)
        silu_gate, at = carve(at, S, F32)
        hidden, at = carve(at, S, F32)
        ht, at = carve(at, 2 * 3 * S)
        ffn_out, at = carve(at, TT * D, F32)
        x_in = x_in.rearrange("p (t d) -> p t d", t=TT)
        ffn_in = ffn_in.rearrange("p (s w n) -> p s w n", s=2, w=3)
        HT = [ht.rearrange("p (a s n) -> p a s n", a=2, s=3)[:, part] for part in (0, 1)]
        ffn_out = ffn_out.rearrange("p (t d) -> p t d", t=TT)
        W, at = carve(0, 2 * group)
        z, at = carve(at, 2 * 2 * HG * S)
        pt, at = carve(at, 2 * PW)
        probs, at = carve(at, PW, F32)
        acc, at = carve(at, (T // P) * D, F32)
        x_again, at = carve(at, 2 * D, F32)
        silu_again, at = carve(at, 2 * D, F32)
        Z = [z.rearrange("p (s b h n) -> p s b h n", s=2, b=2, h=HG)[:, part] for part in (0, 1)]
        PT = [pt.rearrange("p (s n) -> p s n", s=2)[:, part] for part in (0, 1)]
        acc = acc.rearrange("p (t d) -> p t d", d=D)
        x_last, at = carve(0, TT * D, F32)
        silu_last, at = carve(at, TT * D, F32)
        x_last = x_last.rearrange("p (t d) -> p t d", t=TT)
        silu_last = silu_last.rearrange("p (t d) -> p t d", t=TT)
        x_again = x_again.rearrange("p (s d) -> p s d", s=2)
        silu_again = silu_again.rearrange("p (s d) -> p s d", s=2)

        XT = [sb(f"XT_{n}", [P, KT, T], F16) for n in ("hi", "lo")]
        V = [sb(f"V_{n}", [P, 2, TT, HG * E], F16) for n in ("hi", "lo")]
        Q = [sb(f"Q_{n}", [P, S], F16) for n in ("hi", "lo")]
        K = [sb(f"K_{n}", [P, S], F16) for n in ("hi", "lo")]
        w_in = sb("w_in", [P, 2, 512], F32)
        ident = sb("ident", [P, P], F32)
        mask = sb("mask", [P, 2, P], F32)
        cols_in = sb("cols_in", [P, 3 * H + 2 * MT], F32)
        biases = sb("biases", [P, 3 * H], F32)
        ffn_scales = sb("ffn_scales", [P, 2 * MT], F32)
        b_o_rows = sb("b_o_rows", [P, D], F32)
        down_rows = sb("down_rows", [P, D], F32)
        ones = sb("ones", [P, 1], F32)
        lo_abs = sb("lo_abs", [P, 3 * 512], F16)
        lo_sums = sb("lo_sums", [P, MT], F32)
        lo_total = sb("lo_total", [1, 1], F32)
        exact_flag = sb("exact_flag", [1, 1], mybir.dt.int32)
        stats = sb("stats", [P, TT, 6], F32)
        moments = sb("moments", [P, TT, 2], F32)
        var_eps = sb("var_eps", [P, TT], F32)
        std = sb("std", [P, TT], F32)
        rstd0 = sb("rstd0", [P, TT], F32)
        newton_a = sb("newton_a", [P, TT], F32)
        newton_b = sb("newton_b", [P, TT], F32)
        rstd = sb("rstd", [P, TT], F32)
        row_max = sb("row_max", [P, TT], F32)
        neg_max = sb("neg_max", [P, TT], F32)
        row_sum = sb("row_sum", [P, TT], F32)
        inv_sum = sb("inv_sum", [P, TT], F32)

        bank = [ctx.enter_context(nc.psum_tensor(f"bank{i}", [P, 512], F32)) for i in range(8)]
        GATE, UP, XB, DOWN = bank[0], bank[1], bank[2:4], bank[4:8]
        A0, A1, SC, TR = bank[2], bank[3], [bank[0], bank[1], bank[4]], bank[5:8]
        ZB = TR[0]
        LAST = [A1, A0, SC[0], SC[1]]

        def xt_bank(c, k):
            return bank[2 + k] if isinstance(c, int) and c == 0 else XB[k % 2]

        const_loaded = sem("const_loaded")
        const_scaled = sem("const_scaled")
        blank_ok = sem("blank_ok")
        ident_ok = sem("ident_ok")
        x_loaded = [sem(f"x_loaded{i}") for i in range(TT)]
        stats_ok = sem("stats_ok")
        moments_ok = sem("moments_ok")
        var_ok = sem("var_ok")
        std_ok = sem("std_ok")
        rstd_step = sem("rstd_step")
        xn_ok = sem("xn_ok")
        xt_mm = sem("xt_mm")
        xt_hi = sem("xt_hi")
        xt_lo = sem("xt_lo")
        ffn_loaded = [sem("ffn_loaded0"), sem("ffn_loaded1")]
        fw_hi = sem("fw_hi")
        fw_lo = sem("fw_lo")
        lo_summed = sem("lo_summed")
        lo_mm = sem("lo_mm")
        lo_known = sem("lo_known")
        gate_mm = sem("gate_mm")
        up_mm = sem("up_mm")
        gate_silu = sem("gate_silu")
        hidden_ok = sem("hidden_ok")
        ht_hi = sem("ht_hi")
        ht_lo = sem("ht_lo")
        down_mm = sem("down_mm")
        down_scaled = sem("down_scaled")
        down_silu = sem("down_silu")
        park_done = sem("park_done")
        w_loaded = sem("w_loaded")
        w_hi = sem("w_hi")
        w_lo = sem("w_lo")
        a0_mm = sem("a0_mm")
        a1_mm = sem("a1_mm")
        a0_hi = sem("a0_hi")
        a1_hi = sem("a1_hi")
        a0_lo = sem("a0_lo")
        a1_lo = sem("a1_lo")
        score_mm = sem("score_mm")
        masked = sem("masked")
        maxed = sem("maxed")
        negated = sem("negated")
        exp_ok = sem("exp_ok")
        inverted = sem("inverted")
        probs_ok = sem("probs_ok")
        t_mm = sem("t_mm")
        t_hi = sem("t_hi")
        t_lo = sem("t_lo")
        z_mm = sem("z_mm")
        z_hi = sem("z_hi")
        z_lo = sem("z_lo")
        acc_ready = sem("acc_ready")
        tail_loaded = [sem("tail_loaded0"), sem("tail_loaded1")]
        last_loaded = sem("last_loaded")
        base_mul = sem("base_mul")
        base_ok = sem("base_ok")
        last_mm = sem("last_mm")
        last_mul = sem("last_mul")
        last_sum = sem("last_sum")
        last_stored = sem("last_stored")
        tail_mul = sem("tail_mul")
        tail_add = sem("tail_add")
        stored = [sem("stored0"), sem("stored1")]

        def w_at(owner, part, sl, col=0, width=512):
            at = ((owner // SLICES) % 2) * group + (part * SLICES * 512 + sl * 512 + col)
            return W[:, ds(at, width)]

        def head_of(u):
            return (u // SLICES) * HG + u % HG

        def bias_of(kind, u):
            return biases[:, ds(head_of(u) + kind * H, 1)]

        block = ctx.enter_context(nc.Block())

        @block.sync
        def _(sp):
            def load_x(c):
                for t in range(TT):
                    sp.dma_start(x_in[:, t], x_tiles[TT * c + t]).then_inc(x_loaded[t], 16)

            load_x(0)
            for m in range(2):
                sp.dma_start(ffn_in[:, m], ffn_w[m]).then_inc(ffn_loaded[m], 16)
            sp.dma_start(cols_in[:], cols).then_inc(const_loaded, 16)
            sp.dma_start(down_rows[:], down_s.partition_broadcast(P)).then_inc(const_loaded, 16)
            sp.dma_start(b_o_rows[:], b_o.partition_broadcast(P)).then_inc(const_loaded, 16)
            sp.wait_ge(xt_mm, KT)
            load_x(1)
            with sp.Fori(1, MT // 2) as i:
                for par in range(2):
                    sp.wait_ge(fw_lo, 3 * (2 * i + par - 1))
                    sp.dma_start(ffn_in[:, par], ffn_w[2 * i + par]).then_inc(ffn_loaded[par], 16)
            sp.wait_ge(fw_lo, 3 * (MT - 2))
            sp.dma_start(ffn_in[:, 0], ffn_w[MT - 1]).then_inc(ffn_loaded[0], 16)
            for c in range(2, B):
                sp.wait_ge(xt_mm, KT * c)
                load_x(c)
            sp.dma_start(w_in[:, 0], attn_w[0]).then_inc(w_loaded, 16)
            with sp.Fori(1, B * SLICES) as sl:
                sp.wait_ge(w_lo, sl)
                sp.dma_start(w_in[:, sl % 2], attn_w[sl]).then_inc(w_loaded, 16)
            sp.wait_ge(park_done, 16 * B)
            for par in range(2):
                sp.dma_start(x_again[:, par], x_tiles[par]).then_inc(tail_loaded[par], 16)
                sp.dma_start(silu_again[:, par], parked_tiles[par]).then_inc(tail_loaded[par], 16)
            def store(tile, par, i):
                sp.wait_ge(tail_add, tile + 1)
                sp.dma_start(out_tiles[tile], silu_again[:, par]).then_inc(stored[par], 16)

            with sp.Fori(0, TAIL // 2 - 1) as i:
                for par in range(2):
                    store(2 * i + par, par, i)
                    sp.wait_ge(stored[par], 16 * (i + 1))
                    sp.dma_start(x_again[:, par], x_tiles[2 * i + par + 2]).then_inc(tail_loaded[par], 16)
                    sp.dma_start(silu_again[:, par], parked_tiles[2 * i + par + 2]).then_inc(tail_loaded[par], 16)
            sp.wait_ge(a1_lo, a1_before(56, "middle"))
            sp.dma_start(x_last, x_chunks[B - 1]).then_inc(last_loaded, 16)
            sp.dma_start(silu_last, parked_chunks[B - 1]).then_inc(last_loaded, 16)
            for par in range(2):
                store(TAIL - 2 + par, par, TAIL // 2 - 1)
            for t in range(TT):
                sp.wait_ge(last_sum, t + 1)
                sp.dma_start(out_tiles[TAIL + t], silu_last[:, t]).then_inc(last_stored, 16)
            for par in range(2):
                sp.wait_ge(stored[par], 16 * (TAIL // 2))
            sp.wait_ge(last_stored, 16 * TT)

        @block.gpsimd
        def _(pool):
            nc.gpsimd.memset(ident[:], 0.0).then_inc(blank_ok, 1)
            nc.gpsimd.memset(mask[:], 0.0).then_inc(blank_ok, 1)
            nc.gpsimd.memset(ones[:], 1.0).then_inc(ident_ok, 1)
            pool.wait_ge(blank_ok, 2)
            nc.gpsimd.affine_select(out=ident[:], in_=ident[:], compare_op=ALU.not_equal, fill=1.0, base=0,
                                    pattern=[[-1, P]], channel_multiplier=1).then_inc(ident_ok, 1)
            nc.gpsimd.affine_select(out=mask[:], in_=mask[:], compare_op=ALU.is_ge, fill=MASKED, base=0,
                                    pattern=[[0, 2], [-1, P]], channel_multiplier=1).then_inc(ident_ok, 1)
            pool.wait_ge(const_loaded, 48)
            nc.gpsimd.tensor_scalar(ffn_scales[:], cols_in[:, 3 * H:], 1.0 / WS, None, ALU.mult).then_inc(const_scaled, 1)
            nc.gpsimd.tensor_scalar(biases[:], cols_in[:, 0:3 * H], WS, None, ALU.mult).then_inc(const_scaled, 1)
            nc.gpsimd.tensor_scalar(down_rows[:], down_rows[:], 1.0 / WS, None, ALU.mult).then_inc(const_scaled, 1)
            pool.wait_ge(score_mm, 1)
            pool.wait_ge(park_done, 16 * B)
            with pool.Fori(0, T // P) as t:
                nc.gpsimd.tensor_copy(acc[:, t], b_o_rows[:]).then_inc(acc_ready, 1)

            def finish(t, par, turns, adder, added):
                pool.wait_ge(tail_loaded[par], 32 * turns)
                pool.wait_ge(adder, added)
                nc.gpsimd.tensor_tensor(silu_again[:, par], acc[:, t], silu_again[:, par],
                                        ALU.mult).then_inc(tail_mul, 1)
                pool.wait_ge(tail_mul, t + 1)
                nc.gpsimd.tensor_tensor(silu_again[:, par], silu_again[:, par], x_again[:, par],
                                        ALU.add).then_inc(tail_add, 1)

            with pool.Fori(0, 4) as i:
                for par in range(2):
                    finish(2 * i + par, par, i + 1, a1_lo, a1_before(2 * i + par + 53, "middle"))
            for t in range(8, TAIL):
                finish(t, t % 2, t // 2 + 1, a0_lo, a0_before(t + 53) - (t == TAIL - 1))
            pool.wait_ge(last_loaded, 32)
            for t in range(TT):
                nc.gpsimd.tensor_tensor(acc[:, TAIL + t], acc[:, TAIL + t], silu_last[:, t], ALU.mult).then_inc(base_mul, 1)
                pool.wait_ge(base_mul, t + 1)
                nc.gpsimd.tensor_tensor(acc[:, TAIL + t], acc[:, TAIL + t], x_last[:, t], ALU.add).then_inc(base_ok, 1)

        @block.tensor
        def _(pe):
            def product(out, stationary, moving, tiles, first=True, last=True, passes=PASSES):
                for n, k in enumerate(tiles):
                    for i, (a, b) in enumerate(passes):
                        mm = nc.tensor.matmul(out, stationary(a, k), moving(b, k),
                                              start=first and n == 0 and i == 0,
                                              stop=last and n == len(tiles) - 1 and i == len(passes) - 1)
                return mm

            def transpose_x(c, k):
                to = xt_bank(c, k)
                if k >= 2 and to is XB[k % 2]:
                    pe.wait_ge(xt_lo, KT * c + k - 1)
                for t in range(TT):
                    if k == 0:
                        pe.wait_ge(xn_ok, TT * c + t + 1)
                    tr = nc.tensor.transpose(to[:, t * P:(t + 1) * P], x_in[:, t, k * P:(k + 1) * P], ident[:])
                tr.then_inc(xt_mm, 1)

            def project_ffn(bank_, w, c, m, exact, tiles=range(KT), first=True, last=True):
                return product(bank_[:], lambda a, k: FW[a][:, m, w, k * P:(k + 1) * P],
                               lambda b, k: XT[b][:, k, ds(c * S, S)], tiles, first, last,
                               EXACT_STATIONARY if exact else PASSES)

            def down(c, m, slot, tiles, start, stop, exact):
                for t in tiles:
                    if start and not (isinstance(c, int) and c == 0):
                        pe.wait_ge(down_scaled, TT * (c - 1) + t + 1)
                    mm = product(DOWN[t][:], lambda a, _: HT[a][:, slot, t * P:(t + 1) * P],
                                 lambda b, _: FW[b][:, m, 2, :], [0], start, stop,
                                 EXACT_MOVING if exact else PASSES)
                    if stop:
                        mm.then_inc(down_mm, 1)

            def step(c, m, slot, before, exact, split_weights=False):
                n = MT * c + m
                first, final = (isinstance(before[1], int) and before[1] == v for v in (0, MT - 1))
                if split_weights:
                    pe.wait_ge(fw_lo, 3 * m + 3)
                if isinstance(m, int) and m == 0:
                    pe.wait_ge(xt_lo, KT * (c + 1))
                pe.wait_ge(gate_silu, n)
                project_ffn(GATE, 0, c, m, exact).then_inc(gate_mm, 1)
                pe.wait_ge(ht_lo, n)
                down(*before, (0, 1), first, final, exact)
                pe.wait_ge(hidden_ok, n)
                project_ffn(UP, 1, c, m, exact).then_inc(up_mm, 1)
                down(*before, (2, 3), first, final, exact)

            def steps(c, lo, hi, exact, split_weights=False):
                with pe.Fori(lo // 2, hi // 2) as i:
                    for par in range(2):
                        step(c, 2 * i + par, par, (c, 2 * i + par - 1, 1 - par), exact, split_weights)

            def end_chunk(c, exact):
                for k in range(2, KT):
                    transpose_x(c + 1, k)
                step(c, MT - 1, 2, (c, MT - 2, 1), exact)
                step(c + 1, 0, 0, (c, MT - 1, 2), exact)

            def later_chunks(exact):
                step(0, 9, 1, (0, 8, 0), exact)
                end_chunk(0, exact)
                with pe.Fori(1, B - 1) as c:
                    step(c, 1, 1, (c, 0, 0), exact)
                    steps(c, 2, 6, exact)
                    for k in range(2):
                        transpose_x(c + 1, k)
                    steps(c, 6, 10, exact)
                    end_chunk(c, exact)
                step(B - 1, 1, 1, (B - 1, 0, 0), exact)
                steps(B - 1, 2, 10, exact)
                step(B - 1, MT - 1, 2, (B - 1, MT - 2, 1), exact)

            def attention_begins(exact):
                project_head(A0, Q_SL, 0, a0_mm)
                project_head(A1, K_SL, 0, a1_mm)
                pe.wait_ge(a0_lo, 1)
                project_v(A0, 0, a0_mm)
                pe.wait_ge(ht_lo, MT * B)
                down(B - 1, MT - 1, 2, (0, 1), False, True, exact)
                pe.wait_ge(a1_lo, 1)
                project_v(A1, 1, a1_mm)
                down(B - 1, MT - 1, 2, (2, 3), False, True, exact)

            pe.wait_ge(ident_ok, 2)
            for k in range(KT):
                transpose_x(0, k)
            pe.wait_ge(fw_lo, 1)
            for k in range(KT):
                pe.wait_ge(xt_lo, k + 1)
                mm = project_ffn(GATE, 0, 0, 0, False, [k], k == 0, k == KT - 1)
            mm.then_inc(gate_mm, 1)
            pe.wait_ge(fw_lo, 2)
            project_ffn(UP, 1, 0, 0, False).then_inc(up_mm, 1)
            step(0, 1, 1, (0, 0, 0), False, True)
            steps(0, 2, 6, False, True)
            for k in range(2):
                transpose_x(1, k)
            steps(0, 6, 8, False, True)
            pe.wait_ge(lo_summed, MT)
            pe.wait_ge(xt_lo, KT + 1)
            nc.tensor.matmul(XB[0][0:1, 0:MT], ones[:], lo_sums[:], start=True, stop=True).then_inc(lo_mm, 1)
            step(0, 8, 0, (0, 7, 1), False, True)

            def project_head(bank_, sl, n, signal):
                xo = ((n // HG) % B) * S
                product(bank_[:], lambda a, k: w_at(n, a, sl + k, (n % HG) * E, E),
                        lambda b, k: XT[b][:, k, ds(xo, S)], range(KT)).then_inc(signal, 1)

            def project_v(bank_, t, signal):
                product(bank_[:], lambda a, k: XT[a][:, k, ds((t % (T // P)) * P, P)],
                        lambda b, k: w_at(t, b, V_SL + k), range(KT)).then_inc(signal, 1)

            def scores():
                for i, b_, col, _ in SCORE_TILES:
                    width = (i + 1) * P
                    mm = product(SC[b_][:, col:col + width], lambda a, _: Q[a][:, i * P:(i + 1) * P],
                                 lambda b, _: K[b][:, 0:width], [0])
                    if i != 2:
                        mm.then_inc(score_mm, 1)

            def transpose_probs(u):
                pe.wait_ge(probs_ok, u + 1)
                if not (isinstance(u, int) and u == 0):
                    pe.wait_ge(z_lo, u)
                for j, b_, col, _ in KEY_TILES:
                    for i in range(j, TT):
                        at = P_AT[i] + j * P
                        tr = nc.tensor.transpose(TR[b_][:, col + (i - j) * P:col + (i - j + 1) * P],
                                                 probs[:, at:at + P], ident[:])
                    if j != 1:
                        tr.then_inc(t_mm, 1)

            def weigh_v(u):
                for n, (j, b_, _, at) in enumerate(KEY_TILES):
                    pe.wait_ge(t_lo, 3 * u + b_ + 1)
                    mm = product(ZB[:, j * P:], lambda a, _: V[a][:, (u // HG) % 2, j, ds((u % HG) * E, E)],
                                 lambda b, _: PT[b][:, at:at + S - j * P], [0], n == 0, n == TT - 1)
                mm.then_inc(z_mm, 1)

            def project_out(to, t, heads=range(HG), first=True, last=True):
                return product(to, lambda a, j: Z[a][:, (t // TT) % 2, j, ds((t % TT) * P, P)],
                               lambda b, j: w_at(t, b, O_SL + j), heads, first, last)

            def unit(u, when, more_w=True):
                if more_w:
                    pe.wait_ge(w_lo, u + 13)
                pe.wait_ge(a0_lo, a0_before(u))
                project_head(A0, Q_SL, u + 1, a0_mm)
                pe.wait_ge(a1_lo, a1_before(u, when))
                project_head(A1, K_SL, u + 1, a1_mm)
                transpose_probs(u)
                pe.wait_ge(a0_lo, a0_before(u) + 1)
                if when == "late":
                    project_out(A0[:], u - 4).then_inc(a0_mm, 1)
                else:
                    project_v(A0, u + 4, a0_mm)
                pe.wait_ge(a1_lo, a1_before(u, when) + 1)
                scores()
                if when == "middle":
                    project_out(A1[:], u - 4).then_inc(a1_mm, 1)
                weigh_v(u)

            pe.wait_ge(lo_known, 2)
            exact = pe.value_load(exact_flag[:], min_val=0, max_val=1)
            with pe.If(exact):
                later_chunks(True)
                pe.wait_ge(w_lo, SLICES)
                attention_begins(True)
            with pe.Else():
                later_chunks(False)
                pe.wait_ge(w_lo, SLICES)
                attention_begins(False)
            pe.wait_ge(a0_lo, 2)
            project_v(A0, 2, a0_mm)
            pe.wait_ge(down_scaled, TT * (B - 1) + 1)
            scores()
            pe.wait_ge(a1_lo, 2)
            project_v(A1, 3, a1_mm)
            pe.wait_ge(down_scaled, TT * B)
            unit(0, "early")
            with pe.Fori(1, 4) as u:
                unit(u, "early")
            with pe.Fori(4, 48) as u:
                unit(u, "middle")
            pe.wait_ge(w_lo, B * SLICES)
            with pe.Fori(48, 60) as u:
                unit(u, "middle", more_w=False)
            with pe.Fori(60, 63) as u:
                unit(u, "late", more_w=False)
            pe.wait_ge(a0_lo, a0_before(63))
            project_out(A0[:], 59).then_inc(a0_mm, 1)
            transpose_probs(63)
            weigh_v(63)
            pe.wait_ge(a0_lo, a0_before(63) + 1)
            for t in (0, 1):
                project_out(LAST[t][:], 60 + t, range(HG - 1), last=False)
            pe.wait_ge(z_lo, NU)
            for t in (0, 1):
                project_out(LAST[t][:], 60 + t, [HG - 1], first=False).then_inc(last_mm, 1)
            for t in (2, 3):
                project_out(LAST[t][:], 60 + t).then_inc(last_mm, 1)

        @block.scalar
        def _(act):
            def split_ffn(m, par):
                act.wait_ge(ffn_loaded[par], 16 * (m // 2 + 1))
                for w in range(3):
                    nc.scalar.activation(FW[0][:, m, w, :], ffn_in[:, par, w], ACT.Copy, scale=WS).then_inc(fw_hi, 1)
                if not (isinstance(m, int) and m == 0):
                    sum_lo(m - 1)

            def sum_lo(m):
                act.wait_ge(fw_lo, 3 * m + 3)
                if not (isinstance(m, int) and m == 0):
                    act.wait_ge(lo_summed, m)
                nc.scalar.activation(lo_abs[:], FW[1][:, m].rearrange("p w n -> p (w n)"), ACT.Abs,
                                     accum_out=lo_sums[:, ds(m, 1)]).then_inc(lo_summed, 1)

            def split_attn(sl):
                act.wait_ge(w_loaded, 16 * (sl + 1))
                nc.scalar.activation(w_at(sl, 0, sl % SLICES), w_in[:, sl % 2], ACT.Copy, scale=WS).then_inc(w_hi, 1)

            def root(c):
                act.wait_ge(var_ok, c + 1)
                nc.scalar.activation(std[:], var_eps[:], ACT.Sqrt).then_inc(std_ok, 1)

            def split_x(c, k):
                act.wait_ge(xt_mm, KT * c + k + 1)
                nc.scalar.activation(XT[0][:, k, ds(c * S, S)], xt_bank(c, k)[:], ACT.Copy).then_inc(xt_hi, 1)

            def silu_down(c, tiles):
                for t in tiles:
                    act.wait_ge(down_scaled, TT * c + t + 1)
                    nc.scalar.activation(ffn_out[:, t], ffn_out[:, t], ACT.Silu).then_inc(down_silu, 1)

            def park(c):
                act.wait_ge(down_silu, TT * (c + 1))
                act.dma_start(parked_chunks[c], ffn_out).then_inc(park_done, 16)

            def step(c, m, slot, down_of=None):
                n = MT * c + m
                act.wait_ge(gate_mm, n + 1)
                nc.scalar.activation(silu_gate, GATE[:], ACT.Silu, scale=ffn_scales[:, ds(m, 1)]).then_inc(gate_silu, 1)
                if down_of is not None:
                    silu_down(down_of, (0, 1))
                act.wait_ge(hidden_ok, n + 1)
                nc.scalar.activation(HT[0][:, slot], hidden, ACT.Copy).then_inc(ht_hi, 1)
                if down_of is not None:
                    silu_down(down_of, (2, 3))
                    park(down_of)

            def steps(c, lo, hi, ahead=0):
                with act.Fori(lo // 2, hi // 2) as i:
                    for par in range(2):
                        step(c, 2 * i + par, par)
                        if ahead:
                            split_ffn(2 * i + par + ahead, (par + ahead) % 2)
                        if c >= 2:
                            split_attn(2 * i + par - 2 + 8 * (c - 2))

            def end_chunk(c):
                split_x(c + 1, 2)
                split_x(c + 1, 3)
                step(c, MT - 1, 2)
                step(c + 1, 0, 0, down_of=c)

            root(0)
            split_ffn(0, 0)
            for k in range(KT):
                split_x(0, k)
            act.wait_ge(const_scaled, 3)
            split_ffn(1, 1)
            step(0, 0, 0)
            split_ffn(2, 0)
            step(0, 1, 1)
            split_ffn(3, 1)
            root(1)
            steps(0, 2, 4, ahead=2)
            split_ffn(6, 0)
            steps(0, 4, 6, ahead=3)
            split_x(1, 0)
            split_x(1, 1)
            steps(0, 6, 8, ahead=3)
            sum_lo(MT - 1)
            step(0, 8, 0)
            step(0, 9, 1)
            end_chunk(0)
            for c in range(1, B):
                step(c, 1, 1)
                if c < B - 1:
                    root(c + 1)
                    steps(c, 2, 6)
                    split_x(c + 1, 0)
                    split_x(c + 1, 1)
                    steps(c, 6, 10)
                    end_chunk(c)
            steps(B - 1, 2, 10)
            step(B - 1, MT - 1, 2)

            def split_head(kind, n, bank_, to, mm, mm_count, hi):
                act.wait_ge(mm, mm_count)
                nc.scalar.activation(to[0][:], bank_[:], ACT.Identity, bias=bias_of(kind, n)).then_inc(hi, 1)

            def split_v(t, bank_, mm, mm_count, hi):
                act.wait_ge(mm, mm_count)
                nc.scalar.activation(V[0][:, (t // TT) % 2, t % TT, :], bank_[:], ACT.Copy).then_inc(hi, 1)

            def exps(n):
                act.wait_ge(negated, n + 1)
                for i, b_, col, at in SCORE_TILES:
                    width = (i + 1) * P
                    e = nc.scalar.activation(probs[:, at:at + width], SC[b_][:, col:col + width], ACT.Exp,
                                             bias=neg_max[:, i:i + 1], scale=SCORE_SCALE,
                                             accum_out=row_sum[:, i:i + 1])
                e.then_inc(exp_ok, 1)

            def split_probs(u):
                for b_, (at, width) in enumerate(BANK_SPANS):
                    act.wait_ge(t_mm, 3 * u + b_ + 1)
                    nc.scalar.activation(PT[0][:, at:at + width], TR[b_][:, 0:width], ACT.Copy).then_inc(t_hi, 1)

            def split_z(u):
                act.wait_ge(z_mm, u + 1)
                nc.scalar.activation(Z[0][:, (u // HG) % 2, u % HG, :], ZB[:], ACT.Identity,
                                     bias=bias_of(2, u)).then_inc(z_hi, 1)

            def unit(u, when, more_w=True):
                split_head(0, u + 1, A0, Q, a0_mm, a0_before(u) + 1, a0_hi)
                split_head(1, u + 1, A1, K, a1_mm, a1_before(u, when) + 1, a1_hi)
                split_probs(u)
                if when != "late":
                    split_v(u + 4, A0, a0_mm, a0_before(u) + 2, a0_hi)
                if more_w:
                    split_attn(u + SLICES)
                exps(u + 1)
                split_z(u)

            split_head(0, 0, A0, Q, a0_mm, 1, a0_hi)
            split_head(1, 0, A1, K, a1_mm, 1, a1_hi)
            split_v(0, A0, a0_mm, 2, a0_hi)
            silu_down(B - 1, (0, 1))
            split_v(1, A1, a1_mm, 2, a1_hi)
            silu_down(B - 1, (2, 3))
            park(B - 1)
            split_v(2, A0, a0_mm, 3, a0_hi)
            exps(0)
            split_v(3, A1, a1_mm, 3, a1_hi)
            with act.Fori(0, 4) as u:
                unit(u, "early")
            with act.Fori(4, 48) as u:
                unit(u, "middle")
            with act.Fori(48, 60) as u:
                unit(u, "middle", more_w=False)
            with act.Fori(60, 63) as u:
                unit(u, "late", more_w=False)
            split_probs(63)
            split_z(63)

        @block.vector
        def _(dve):
            def split_ffn(m, par, parts=range(3)):
                for w in parts:
                    dve.wait_ge(fw_hi, 3 * m + w + 1)
                    nc.vector.scalar_tensor_tensor(out=FW[1][:, m, w, :], in0=ffn_in[:, par, w], scalar=WS,
                                                   in1=FW[0][:, m, w, :], op0=ALU.mult,
                                                   op1=ALU.subtract).then_inc(fw_lo, 1)

            def split_attn(sl):
                dve.wait_ge(w_hi, sl + 1)
                nc.vector.scalar_tensor_tensor(out=w_at(sl, 1, sl % SLICES), in0=w_in[:, sl % 2], scalar=WS,
                                               in1=w_at(sl, 0, sl % SLICES), op0=ALU.mult,
                                               op1=ALU.subtract).then_inc(w_lo, 1)

            def normalise(c):
                for t in range(TT):
                    dve.wait_ge(x_loaded[t], 16 * (c + 1))
                    nc.vector.bn_stats(out=stats[:, t], in_=x_in[:, t]).then_inc(stats_ok, 1)
                for t in range(TT):
                    dve.wait_ge(stats_ok, TT * c + t + 1)
                    nc.vector.bn_aggr(out=moments[:, t], in_=stats[:, t]).then_inc(moments_ok, 1)
                dve.wait_ge(moments_ok, TT * (c + 1))
                nc.vector.tensor_scalar(var_eps[:], moments[:, :, 1], EPS, None, ALU.add).then_inc(var_ok, 1)
                dve.wait_ge(std_ok, c + 1)
                nc.vector.reciprocal(rstd0[:], std[:]).then_inc(rstd_step, 1)
                dve.wait_ge(rstd_step, 4 * c + 1)
                nc.vector.tensor_tensor(newton_a[:], rstd0[:], rstd0[:], ALU.mult).then_inc(rstd_step, 1)
                dve.wait_ge(rstd_step, 4 * c + 2)
                nc.vector.scalar_tensor_tensor(out=newton_b[:], in0=newton_a[:], scalar=-0.5, in1=var_eps[:],
                                               op0=ALU.mult, op1=ALU.mult).then_inc(rstd_step, 1)
                dve.wait_ge(rstd_step, 4 * c + 3)
                nc.vector.scalar_tensor_tensor(out=rstd[:], in0=newton_b[:], scalar=1.5, in1=rstd0[:],
                                               op0=ALU.add, op1=ALU.mult).then_inc(rstd_step, 1)
                dve.wait_ge(rstd_step, 4 * c + 4)
                for t in range(TT):
                    nc.vector.tensor_scalar(x_in[:, t], x_in[:, t], moments[:, t, 0:1], rstd[:, t:t + 1],
                                            ALU.subtract, ALU.mult).then_inc(xn_ok, 1)

            def split_x(c, k):
                dve.wait_ge(xt_hi, KT * c + k + 1)
                nc.vector.tensor_tensor(XT[1][:, k, ds(c * S, S)], xt_bank(c, k)[:], XT[0][:, k, ds(c * S, S)],
                                        ALU.subtract).then_inc(xt_lo, 1)

            def scale_down(c, tiles):
                for t in tiles:
                    dve.wait_ge(down_mm, TT * c + t + 1)
                    if t == 0 and not (isinstance(c, int) and c == 0):
                        dve.wait_ge(park_done, 16 * c)
                    nc.vector.tensor_tensor(ffn_out[:, t], DOWN[t][:], down_rows[:], ALU.mult).then_inc(down_scaled, 1)

            def step(c, m, slot, down_of=None):
                n = MT * c + m
                if down_of is not None:
                    scale_down(down_of, (0, 1))
                dve.wait_ge(gate_silu, n + 1)
                dve.wait_ge(up_mm, n + 1)
                nc.vector.scalar_tensor_tensor(out=hidden, in0=UP[:], scalar=ffn_scales[:, ds(MT + m, 1)],
                                               in1=silu_gate, op0=ALU.mult, op1=ALU.mult).then_inc(hidden_ok, 1)
                dve.wait_ge(ht_hi, n + 1)
                nc.vector.tensor_tensor(HT[1][:, slot], hidden, HT[0][:, slot], ALU.subtract).then_inc(ht_lo, 1)
                if down_of is not None:
                    scale_down(down_of, (2, 3))

            def steps(c, lo, hi, ahead=0):
                with dve.Fori(lo // 2, hi // 2) as i:
                    for par in range(2):
                        step(c, 2 * i + par, par)
                        if ahead:
                            split_ffn(2 * i + par + ahead, (par + ahead) % 2)
                        if c >= 2:
                            split_attn(2 * i + par - 2 + 8 * (c - 2))

            def end_chunk(c):
                split_x(c + 1, 2)
                split_x(c + 1, 3)
                step(c, MT - 1, 2)
                step(c + 1, 0, 0, down_of=c)

            normalise(0)
            split_ffn(0, 0, [0])
            for k in range(KT):
                split_x(0, k)
            split_ffn(0, 0, [1, 2])
            dve.wait_ge(const_scaled, 3)
            split_ffn(1, 1)
            step(0, 0, 0)
            split_ffn(2, 0)
            step(0, 1, 1)
            split_ffn(3, 1)
            normalise(1)
            steps(0, 2, 4, ahead=2)
            split_ffn(6, 0)
            steps(0, 4, 6, ahead=3)
            split_x(1, 0)
            split_x(1, 1)
            steps(0, 6, 8, ahead=3)
            dve.wait_ge(lo_mm, 1)
            nc.vector.tensor_reduce(lo_total[:], XB[0][0:1, 0:MT], AX_X, ALU.add).then_inc(lo_known, 1)
            dve.wait_ge(lo_known, 1)
            nc.vector.tensor_scalar(exact_flag[:], lo_total[:], 0.0, None, ALU.is_equal).then_inc(lo_known, 1)
            step(0, 8, 0)
            step(0, 9, 1)
            end_chunk(0)
            for c in range(1, B):
                step(c, 1, 1)
                if c < B - 1:
                    normalise(c + 1)
                    steps(c, 2, 6)
                    split_x(c + 1, 0)
                    split_x(c + 1, 1)
                    steps(c, 6, 10)
                    end_chunk(c)
            steps(B - 1, 2, 10)
            step(B - 1, MT - 1, 2)

            def split_head(kind, n, bank_, to, hi, hi_count, lo):
                dve.wait_ge(hi, hi_count)
                nc.vector.scalar_tensor_tensor(out=to[1][:], in0=bank_[:], scalar=bias_of(kind, n), in1=to[0][:],
                                               op0=ALU.add, op1=ALU.subtract).then_inc(lo, 1)

            def split_v(t, bank_, hi, hi_count, lo):
                dve.wait_ge(hi, hi_count)
                at = (t // TT) % 2
                nc.vector.tensor_tensor(V[1][:, at, t % TT, :], bank_[:], V[0][:, at, t % TT, :],
                                        ALU.subtract).then_inc(lo, 1)

            def maxima(n):
                for b_, col, blocks in DIAGONALS:
                    dve.wait_ge(score_mm, 3 * n + b_ + 1)
                    nc.vector.tensor_tensor(SC[b_][:, col:col + blocks * P], SC[b_][:, col:col + blocks * P],
                                            mask[:, 0:blocks, :].rearrange("p b k -> p (b k)"),
                                            ALU.add).then_inc(masked, 1)
                dve.wait_ge(masked, 3 * n + 3)
                for i, b_, col, _ in SCORE_TILES:
                    r = nc.vector.reduce_max(row_max[:, i:i + 1], SC[b_][:, col:col + (i + 1) * P], AX_X)
                r.then_inc(maxed, 1)
                dve.wait_ge(maxed, n + 1)
                nc.vector.tensor_scalar(neg_max[:], row_max[:], -SCORE_SCALE, None, ALU.mult).then_inc(negated, 1)

            def normalise_probs(n):
                dve.wait_ge(exp_ok, n + 1)
                nc.vector.reciprocal(inv_sum[:], row_sum[:]).then_inc(inverted, 1)
                dve.wait_ge(inverted, n + 1)
                for i, _, _, at in SCORE_TILES:
                    r = nc.vector.tensor_scalar(probs[:, at:at + (i + 1) * P], probs[:, at:at + (i + 1) * P],
                                                inv_sum[:, i:i + 1], None, ALU.mult)
                r.then_inc(probs_ok, 1)

            def split_probs(u):
                for b_, (at, width) in enumerate(BANK_SPANS):
                    dve.wait_ge(t_hi, 3 * u + b_ + 1)
                    nc.vector.tensor_tensor(PT[1][:, at:at + width], TR[b_][:, 0:width], PT[0][:, at:at + width],
                                            ALU.subtract).then_inc(t_lo, 1)

            def split_z(u):
                dve.wait_ge(z_hi, u + 1)
                at = (u // HG) % 2
                nc.vector.scalar_tensor_tensor(out=Z[1][:, at, u % HG, :], in0=ZB[:], scalar=bias_of(2, u),
                                               in1=Z[0][:, at, u % HG, :], op0=ALU.add,
                                               op1=ALU.subtract).then_inc(z_lo, 1)

            def add_out(t, bank_, mm, mm_count, lo):
                dve.wait_ge(mm, mm_count)
                o = t % (T // P)
                nc.vector.scalar_tensor_tensor(out=acc[:, o], in0=bank_[:], scalar=WS ** -2, in1=acc[:, o],
                                               op0=ALU.mult, op1=ALU.add).then_inc(lo, 1)

            def unit(u, when, more_w=True):
                split_head(0, u + 1, A0, Q, a0_hi, u + 64 if when == "late" else a0_before(u) + 1, a0_lo)
                split_head(1, u + 1, A1, K, a1_hi, 4 + u, a1_lo)
                split_probs(u)
                if when == "late":
                    add_out(u - 4, A0, a0_mm, a0_before(u) + 2, a0_lo)
                else:
                    split_v(u + 4, A0, a0_hi, a0_before(u) + 2, a0_lo)
                if more_w:
                    split_attn(u + SLICES)
                maxima(u + 1)
                if when == "middle":
                    add_out(u - 4, A1, a1_mm, a1_before(u, when) + 2, a1_lo)
                normalise_probs(u + 1)
                split_z(u)

            split_head(0, 0, A0, Q, a0_hi, 1, a0_lo)
            split_head(1, 0, A1, K, a1_hi, 1, a1_lo)
            split_v(0, A0, a0_hi, 2, a0_lo)
            scale_down(B - 1, (0, 1))
            split_v(1, A1, a1_hi, 2, a1_lo)
            scale_down(B - 1, (2, 3))
            split_v(2, A0, a0_hi, 3, a0_lo)
            dve.wait_ge(ident_ok, 2)
            maxima(0)
            split_v(3, A1, a1_hi, 3, a1_lo)
            normalise_probs(0)
            with dve.Fori(0, 4) as u:
                unit(u, "early")
            dve.wait_ge(acc_ready, T // P)
            with dve.Fori(4, 48) as u:
                unit(u, "middle")
            with dve.Fori(48, 60) as u:
                unit(u, "middle", more_w=False)
            with dve.Fori(60, 63) as u:
                unit(u, "late", more_w=False)
            add_out(59, A0, a0_mm, a0_before(63) + 1, a0_lo)
            split_probs(63)
            split_z(63)
            for t in range(TT):
                if t == 0:
                    dve.wait_ge(base_ok, TT)
                dve.wait_ge(last_mm, t + 1)
                nc.vector.scalar_tensor_tensor(out=silu_last[:, t], in0=LAST[t][:], scalar=WS ** -2,
                                               in1=silu_last[:, t], op0=ALU.mult, op1=ALU.mult).then_inc(last_mul, 1)
                dve.wait_ge(last_mul, t + 1)
                nc.vector.tensor_tensor(silu_last[:, t], silu_last[:, t], acc[:, TAIL + t],
                                        ALU.add).then_inc(last_sum, 1)


def kernel(L0_attn_x, L0_attn_W_Q, L0_attn_W_K, L0_attn_W_V, L0_attn_W_O, L0_attn_b_Q, L0_attn_b_K, L0_attn_b_V,
           L0_attn_b_O, L0_ffn_gate_w, L0_ffn_up_w, L0_ffn_down_w, L0_ffn_gate_s, L0_ffn_up_s, L0_ffn_down_s):
    import numpy as np
    import concourse.bacc as bacc
    from concourse.bass_utils import run_bass_kernel_spmd

    x = np.ascontiguousarray(L0_attn_x).reshape(T, D)

    def up_like(w):
        return np.asarray(w).reshape(MT, P, KT, P).transpose(0, 3, 2, 1).reshape(MT, P, 1, 512)
    down = np.asarray(L0_ffn_down_w).T.reshape(MT, P, 1, D)
    ffn_w = np.ascontiguousarray(np.concatenate([up_like(L0_ffn_gate_w), up_like(L0_ffn_up_w), down], axis=2))

    def by_feature(w):
        return np.asarray(w).reshape(H // HG, HG, KT, P, E).transpose(0, 2, 3, 1, 4).reshape(H // HG, KT, P, HG * E)
    w_o = np.asarray(L0_attn_W_O).reshape(H // HG, HG, E, D)
    attn_w = np.ascontiguousarray(np.concatenate(
        [by_feature(L0_attn_W_V), by_feature(L0_attn_W_Q), by_feature(L0_attn_W_K), w_o], axis=1)).reshape(-1, P, 512)

    cols = np.ascontiguousarray(np.concatenate(
        [np.asarray(b).T for b in (L0_attn_b_Q, L0_attn_b_K, L0_attn_b_V)]
        + [np.asarray(v).reshape(MT, P).T for v in (L0_ffn_gate_s, L0_ffn_up_s)], axis=1))

    arrays = {"x": x, "ffn_w": ffn_w, "attn_w": attn_w, "cols": cols,
              "b_o": np.ascontiguousarray(L0_attn_b_O), "down_s": np.ascontiguousarray(L0_ffn_down_s)}
    nc = bacc.Bacc("TRN2", target_bir_lowering=False, num_devices=1)
    args = [nc.dram_tensor(f"{n}_dram", a.shape, F32, kind="ExternalInput").ap() for n, a in arrays.items()]
    out = nc.dram_tensor("out_dram", (T, D), F32, kind="ExternalOutput").ap()
    build(nc, *args, out)
    r = run_bass_kernel_spmd(nc, [{f"{n}_dram": a for n, a in arrays.items()}], core_ids=[0])
    return r.results[0]["out_dram"].reshape(B, S, D)
```

```python
from contextlib import ExitStack

import concourse.bass as bass
from concourse import mybir

ALU = mybir.AluOpType
ACT = mybir.ActivationFunctionType
AX_X = mybir.AxisListType.X
F32 = mybir.dt.float32
F16 = mybir.dt.float16
ds = bass.ds

P = 128
B, S, D = 4, 512, 512
T = B * S
H, E = 16, 128
F = 1408
KT = D // P
TT = S // P
MT = F // P
HG = 4
NU = B * H
TAIL = T // P - TT
TAIL_ADDED = (H // HG - 1) * (T // P)
SLICES = 4 * KT
V_SL, Q_SL, K_SL, O_SL = 0, KT, 2 * KT, 3 * KT
WS = 16.0
SCORE_SCALE = float(E) ** -0.5 / WS ** 2
MASKED = -1.0e5 / SCORE_SCALE
EPS = 1e-5

SCORE_TILES = [(3, 0, 0, 0), (2, 1, 0, 512), (0, 1, 384, 896), (1, 2, 0, 1024)]
P_AT = {i: at for i, _, _, at in SCORE_TILES}
DIAGONALS = [(0, 384, 1), (1, 256, 2), (2, 128, 1)]
J_STEP = TT - 1
PB = J_STEP * (TT - 1) + TT
GAPS = [(7, 1), (10, 2)]
PW = 1280

AHEAD = [(2, 3), (4, 5), (6,), (7,), (8,), (9,), (10,), (), (), ()]
SUMMED_BEFORE = [(), (3,), (4,), (), (), (), (), (), (), ()]
SUMMED_BEHIND = [(2,), (), (5,), (6,), (7,), (8,), (9,), (), (10,), ()]
DVE_LO = 1
FIRST_CHECKED = 2

PASSES = ((0, 0), (0, 1), (1, 0))
EXACT_STATIONARY = ((0, 0), (0, 1))
EXACT_MOVING = ((0, 0), (1, 0))


def build(nc, x, ffn_w, attn_w, cols, b_o, down_s, out):
    x_chunks = x.rearrange("(c t p) d -> c p t d", t=TT, p=P)
    x_tiles = x.rearrange("(t p) d -> t p d", p=P)
    out_tiles = out.rearrange("(t p) d -> t p d", p=P)
    parked = nc.dram_tensor("parked_silu", (T, D), F32, kind="Internal").ap()
    parked_chunks = parked.rearrange("(c t p) d -> c p t d", t=TT, p=P)
    parked_tiles = parked.rearrange("(t p) d -> t p d", p=P)

    with ExitStack() as ctx:
        def sb(name, shape, dt):
            return ctx.enter_context(nc.sbuf_tensor(name, shape, dt))

        def sem(name):
            return ctx.enter_context(nc.semaphore(name))

        group = 2 * SLICES * 512
        arena = sb("arena", [P, 69632], F16)

        def carve(at, size, dt=F16):
            part = arena[:, at:at + size * (2 if dt == F32 else 1)]
            return (part.bitcast(F32) if dt == F32 else part), at + size * (2 if dt == F32 else 1)

        fw, at = carve(group, 2 * MT * 3 * 512)
        FW = [fw.rearrange("p (s m w n) -> p s m w n", s=2, m=MT, w=3)[:, part] for part in (0, 1)]
        x_in, at = carve(at, TT * D, F32)
        ffn_in, at = carve(at, 2 * 3 * 512, F32)
        silu_gate, at = carve(at, S, F32)
        hidden, at = carve(at, S, F32)
        ht, at = carve(at, 2 * 3 * S)
        ffn_out, at = carve(at, TT * D, F32)
        x_in = x_in.rearrange("p (t d) -> p t d", t=TT)
        ffn_in = ffn_in.rearrange("p (s w n) -> p s w n", s=2, w=3)
        HT = [ht.rearrange("p (a s n) -> p a s n", a=2, s=3)[:, part] for part in (0, 1)]
        ffn_out = ffn_out.rearrange("p (t d) -> p t d", t=TT)
        W, at = carve(0, 2 * group)
        z, at = carve(at, 2 * 2 * HG * S)
        p_split, at = carve(at, 2 * PB * P)
        pt, at = carve(at, 2 * PB * P)
        probs, at = carve(at, PW, F32)
        acc, at = carve(at, (T // P) * D, F32)
        Z = [z.rearrange("p (s b h n) -> p s b h n", s=2, b=2, h=HG)[:, part] for part in (0, 1)]
        P_SPLIT = [p_split.rearrange("p (s b k) -> p s b k", s=2, k=P)[:, part] for part in (0, 1)]
        PT = [pt.rearrange("p (s b q) -> p s b q", s=2, q=P)[:, part] for part in (0, 1)]

        def probs_by_block(i, at):
            return probs[:, at:at + (i + 1) * P].rearrange("p (j k) -> p j k", k=P)

        def query_blocks(part, i):
            return P_SPLIT[part][:, i:i + J_STEP * i + 1:J_STEP, :]

        acc = acc.rearrange("p (t d) -> p t d", d=D)
        x_last, at = carve(0, TT * D, F32)
        silu_last, at = carve(at, TT * D, F32)
        x_again, at = carve(at, 2 * D, F32)
        silu_again, at = carve(at, 2 * D, F32)
        x_last = x_last.rearrange("p (t d) -> p t d", t=TT)
        silu_last = silu_last.rearrange("p (t d) -> p t d", t=TT)
        x_again = x_again.rearrange("p (s d) -> p s d", s=2)
        silu_again = silu_again.rearrange("p (s d) -> p s d", s=2)

        XT = [sb(f"XT_{n}", [P, KT, T], F16) for n in ("hi", "lo")]
        V = [sb(f"V_{n}", [P, 2, TT, HG * E], F16) for n in ("hi", "lo")]
        Q = [sb(f"Q_{n}", [P, S], F16) for n in ("hi", "lo")]
        K = [sb(f"K_{n}", [P, S], F16) for n in ("hi", "lo")]
        w_in = sb("w_in", [P, 2, 512], F32)
        ident = sb("ident", [P, P], F32)
        mask = sb("mask", [P, 2, P], F32)
        cols_in = sb("cols_in", [P, 3 * H + 2 * MT], F32)
        biases = sb("biases", [P, 3 * H], F32)
        ffn_scales = sb("ffn_scales", [P, 2 * MT], F32)
        b_o_rows = sb("b_o_rows", [P, D], F32)
        down_rows = sb("down_rows", [P, D], F32)
        ones = sb("ones", [P, 1], F32)
        lo_abs = sb("lo_abs", [P, 3 * 512], F16)
        lo_sums = sb("lo_sums", [P, MT], F32)
        lo_total = sb("lo_total", [1, 1], F32)
        exact_flag = sb("exact_flag", [1, 1], mybir.dt.int32)
        stats = sb("stats", [P, TT, 6], F32)
        moments = sb("moments", [P, TT, 2], F32)
        var_eps = sb("var_eps", [P, TT], F32)
        std = sb("std", [P, TT], F32)
        rstd0 = sb("rstd0", [P, TT], F32)
        newton_a = sb("newton_a", [P, TT], F32)
        newton_b = sb("newton_b", [P, TT], F32)
        rstd = sb("rstd", [P, TT], F32)
        row_max = sb("row_max", [P, TT], F32)
        neg_max = sb("neg_max", [P, TT], F32)
        row_sum = sb("row_sum", [P, TT], F32)
        inv_sum = sb("inv_sum", [P, TT], F32)

        bank = [ctx.enter_context(nc.psum_tensor(f"bank{i}", [P, 512], F32)) for i in range(8)]
        GATE, UP, XB, DOWN = bank[0], bank[1], bank[2:4], bank[4:8]
        QB, KB, VB, OB = bank[2], bank[3], bank[1], bank[7]
        SC, ZB = [bank[0], bank[4], bank[5]], bank[6]
        LAST = [QB, KB, VB, OB]
        LAST_Z = [bank[4], bank[5]]

        def v_bank(t):
            return SC[0] if isinstance(t, int) and t == 1 else VB

        def xt_bank(c, k):
            return bank[2 + k] if isinstance(c, int) and c == 0 else XB[k % 2]

        const_loaded = sem("const_loaded")
        const_scaled = sem("const_scaled")
        blank_ok = sem("blank_ok")
        ident_ok = sem("ident_ok")
        x_loaded = [sem(f"x_loaded{i}") for i in range(TT)]
        stats_ok = sem("stats_ok")
        moments_ok = sem("moments_ok")
        var_ok = sem("var_ok")
        std_ok = sem("std_ok")
        rstd_step = sem("rstd_step")
        xn_ok = sem("xn_ok")
        xt_mm = sem("xt_mm")
        xt_hi = sem("xt_hi")
        xt_lo = sem("xt_lo")
        ffn_loaded = [sem("ffn_loaded0"), sem("ffn_loaded1")]
        fw_hi = sem("fw_hi")
        fw_lo = sem("fw_lo")
        lo_summed = sem("lo_summed")
        lo_maxed = sem("lo_maxed")
        lo_mm = sem("lo_mm")
        lo_known = sem("lo_known")
        branching = sem("branching")
        gate_mm = sem("gate_mm")
        up_mm = sem("up_mm")
        gate_silu = sem("gate_silu")
        hidden_ok = sem("hidden_ok")
        ht_hi = sem("ht_hi")
        ht_lo = sem("ht_lo")
        down_mm = sem("down_mm")
        down_scaled = sem("down_scaled")
        down_silu = sem("down_silu")
        park_done = sem("park_done")
        w_loaded = sem("w_loaded")
        w_hi = sem("w_hi")
        w_lo = sem("w_lo")
        q_mm = sem("q_mm")
        q_hi = sem("q_hi")
        q_lo = sem("q_lo")
        k_mm = sem("k_mm")
        k_hi = sem("k_hi")
        k_lo = sem("k_lo")
        v_mm = sem("v_mm")
        v_hi = sem("v_hi")
        v_lo = sem("v_lo")
        out_mm = sem("out_mm")
        out_added = sem("out_added")
        score_mm = sem("score_mm")
        masked = sem("masked")
        maxed = sem("maxed")
        negated = sem("negated")
        exp_ok = sem("exp_ok")
        inverted = sem("inverted")
        p_hi = sem("p_hi")
        p_lo = sem("p_lo")
        gaps_ok = sem("gaps_ok")
        transposing = sem("transposing")
        pt_ok = [sem("pt_hi_ok"), sem("pt_lo_ok")]
        z_mm = sem("z_mm")
        z_hi = sem("z_hi")
        z_lo = sem("z_lo")
        acc_ready = sem("acc_ready")
        tail_loaded = [sem("tail_loaded0"), sem("tail_loaded1")]
        last_loaded = sem("last_loaded")
        base_mul = sem("base_mul")
        base_ok = sem("base_ok")
        last_mm = sem("last_mm")
        last_mul = sem("last_mul")
        pool_sum = sem("pool_sum")
        last_sum = sem("last_sum")
        last_stored = sem("last_stored")
        tail_mul = sem("tail_mul")
        tail_add = sem("tail_add")
        stored = [sem("stored0"), sem("stored1")]

        def w_at(owner, part, sl, col=0, width=512):
            at = ((owner // SLICES) % 2) * group + (part * SLICES * 512 + sl * 512 + col)
            return W[:, ds(at, width)]

        def head_of(u):
            return (u // SLICES) * HG + u % HG

        def bias_of(kind, u):
            return biases[:, ds(head_of(u) + kind * H, 1)]

        def last_z_part(part, half):
            u = NU - 1
            return Z[part][:, (u // HG) % 2, u % HG, half * 2 * P:(half + 1) * 2 * P]

        block = ctx.enter_context(nc.Block())

        @block.sync
        def _(sp):
            def load_x(c):
                for t in range(TT):
                    sp.dma_start(x_in[:, t], x_tiles[TT * c + t]).then_inc(x_loaded[t], 16)

            load_x(0)
            for m in range(2):
                sp.dma_start(ffn_in[:, m], ffn_w[m]).then_inc(ffn_loaded[m], 16)
            sp.dma_start(cols_in[:], cols).then_inc(const_loaded, 16)
            sp.dma_start(down_rows[:], down_s.partition_broadcast(P)).then_inc(const_loaded, 16)
            sp.dma_start(b_o_rows[:], b_o.partition_broadcast(P)).then_inc(const_loaded, 16)

            def load_ffn(m, par):
                sp.wait_ge(fw_lo, 3 * (m - 1))
                sp.dma_start(ffn_in[:, par], ffn_w[m]).then_inc(ffn_loaded[par], 16)

            load_ffn(2, 0)
            load_ffn(3, 1)
            sp.wait_ge(xt_mm, KT)
            load_x(1)
            with sp.Fori(2, MT // 2) as i:
                for par in range(2):
                    load_ffn(2 * i + par, par)
            load_ffn(MT - 1, 0)
            for c in range(2, B):
                sp.wait_ge(xt_mm, KT * c)
                load_x(c)
            sp.dma_start(w_in[:, 0], attn_w[0]).then_inc(w_loaded, 16)
            with sp.Fori(1, SLICES + 1) as sl:
                sp.wait_ge(w_lo, sl)
                sp.dma_start(w_in[:, sl % 2], attn_w[sl]).then_inc(w_loaded, 16)

            def transpose_probs(n):
                if isinstance(n, int) and n == 0:
                    sp.wait_ge(gaps_ok, 2 * len(GAPS))
                else:
                    sp.wait_ge(z_mm, n)
                for part, split in ((0, p_hi), (1, p_lo)):
                    sp.wait_ge(split, TT * (n + 1))
                    sp.sem_inc(transposing, 1)
                    sp.dma_start_transpose(out=PT[part], in_=P_SPLIT[part].rearrange("p b k -> p (b k)")
                                           ).then_inc(pt_ok[part], 16)

            transpose_probs(0)
            with sp.Fori(SLICES + 1, B * SLICES) as sl:
                sp.wait_ge(w_lo, sl)
                sp.dma_start(w_in[:, sl % 2], attn_w[sl]).then_inc(w_loaded, 16)
                transpose_probs(sl - SLICES)
            with sp.Fori((B - 1) * SLICES, NU) as n:
                transpose_probs(n)
            for t in range(TT):
                sp.wait_ge(pool_sum if t < 2 else last_sum, t % 2 + 1)
                sp.dma_start(out_tiles[TAIL + t], silu_last[:, t]).then_inc(last_stored, 16)
            sp.wait_ge(last_stored, 16 * TT)

        @block.gpsimd
        def _(pool):
            nc.gpsimd.memset(ident[:], 0.0).then_inc(blank_ok, 1)
            nc.gpsimd.memset(mask[:], 0.0).then_inc(blank_ok, 1)
            nc.gpsimd.memset(ones[:], 1.0).then_inc(ident_ok, 1)
            pool.wait_ge(blank_ok, 2)
            nc.gpsimd.affine_select(out=ident[:], in_=ident[:], compare_op=ALU.not_equal, fill=1.0, base=0,
                                    pattern=[[-1, P]], channel_multiplier=1).then_inc(ident_ok, 1)
            nc.gpsimd.affine_select(out=mask[:], in_=mask[:], compare_op=ALU.is_ge, fill=MASKED, base=0,
                                    pattern=[[0, 2], [-1, P]], channel_multiplier=1).then_inc(ident_ok, 1)
            pool.wait_ge(const_loaded, 48)
            nc.gpsimd.tensor_scalar(ffn_scales[:], cols_in[:, 3 * H:], 1.0 / WS, None, ALU.mult).then_inc(const_scaled, 1)
            nc.gpsimd.tensor_scalar(biases[:], cols_in[:, 0:3 * H], WS, None, ALU.mult).then_inc(const_scaled, 1)
            nc.gpsimd.tensor_scalar(down_rows[:], down_rows[:], 1.0 / WS, None, ALU.mult).then_inc(const_scaled, 1)
            pool.wait_ge(score_mm, 1)
            for part in (0, 1):
                for at, blocks in GAPS:
                    nc.gpsimd.memset(P_SPLIT[part][:, at:at + blocks, :], 0.0).then_inc(gaps_ok, 1)
            pool.wait_ge(park_done, 16 * B)
            with pool.Fori(0, T // P) as t:
                nc.gpsimd.tensor_copy(acc[:, t], b_o_rows[:]).then_inc(acc_ready, 1)

            def load_tail(t, par):
                pool.dma_start(x_again[:, par], x_tiles[t]).then_inc(tail_loaded[par], 16)
                pool.dma_start(silu_again[:, par], parked_tiles[t]).then_inc(tail_loaded[par], 16)

            def finish(t, par, turns):
                pool.wait_ge(tail_loaded[par], 32 * turns)
                pool.wait_ge(out_added, TAIL_ADDED + t + 1)
                nc.gpsimd.tensor_tensor(silu_again[:, par], acc[:, t], silu_again[:, par],
                                        ALU.mult).then_inc(tail_mul, 1)
                pool.wait_ge(tail_mul, t + 1)
                nc.gpsimd.tensor_tensor(silu_again[:, par], silu_again[:, par], x_again[:, par],
                                        ALU.add).then_inc(tail_add, 1)
                pool.wait_ge(tail_add, t + 1)
                pool.dma_start(out_tiles[t], silu_again[:, par]).then_inc(stored[par], 16)

            def refill(t, par, turns):
                pool.wait_ge(stored[par], 16 * turns)
                load_tail(t, par)

            pool.wait_ge(v_mm, TAIL_ADDED)
            pool.wait_ge(q_mm, TAIL_ADDED)
            for par in range(2):
                load_tail(par, par)
            with pool.Fori(0, TT // 2) as i:
                for par in range(2):
                    finish(2 * i + par, par, i + 1)
                    refill(2 * i + par + 2, par, i + 1)
            pool.dma_start(x_last, x_chunks[B - 1]).then_inc(last_loaded, 16)
            pool.dma_start(silu_last, parked_chunks[B - 1]).then_inc(last_loaded, 16)
            with pool.Fori(TT // 2, TT) as i:
                for par in range(2):
                    finish(2 * i + par, par, i + 1)
                    refill(2 * i + par + 2, par, i + 1)
            pool.wait_ge(last_loaded, 32)
            for t in range(TT):
                nc.gpsimd.tensor_tensor(acc[:, TAIL + t], acc[:, TAIL + t], silu_last[:, t], ALU.mult).then_inc(base_mul, 1)
                pool.wait_ge(base_mul, t + 1)
                nc.gpsimd.tensor_tensor(acc[:, TAIL + t], acc[:, TAIL + t], x_last[:, t], ALU.add).then_inc(base_ok, 1)
            for par in range(2):
                finish(2 * TT + par, par, TT + 1)
                refill(2 * TT + par + 2, par, TT + 1)
            for par in range(2):
                finish(TAIL - 2 + par, par, TAIL // 2)
            for t in (0, 1):
                pool.wait_ge(last_mul, t + 1)
                nc.gpsimd.tensor_tensor(silu_last[:, t], silu_last[:, t], acc[:, TAIL + t],
                                        ALU.add).then_inc(pool_sum, 1)
            for par in range(2):
                pool.wait_ge(stored[par], 16 * (TAIL // 2))

        @block.tensor
        def _(pe):
            def product(out, stationary, moving, tiles, first=True, last=True, passes=PASSES):
                for n, k in enumerate(tiles):
                    for i, (a, b) in enumerate(passes):
                        mm = nc.tensor.matmul(out, stationary(a, k), moving(b, k),
                                              start=first and n == 0 and i == 0,
                                              stop=last and n == len(tiles) - 1 and i == len(passes) - 1)
                return mm

            def transpose_x(c, k):
                to = xt_bank(c, k)
                if k >= 2 and to is XB[k % 2]:
                    pe.wait_ge(xt_lo, KT * c + k - 1)
                for t in range(TT):
                    if k == 0:
                        pe.wait_ge(xn_ok, TT * c + t + 1)
                    tr = nc.tensor.transpose(to[:, t * P:(t + 1) * P], x_in[:, t, k * P:(k + 1) * P], ident[:])
                tr.then_inc(xt_mm, 1)

            def project_ffn(bank_, w, c, m, exact, tiles=range(KT), first=True, last=True):
                return product(bank_[:], lambda a, k: FW[a][:, m, w, k * P:(k + 1) * P],
                               lambda b, k: XT[b][:, k, ds(c * S, S)], tiles, first, last,
                               EXACT_STATIONARY if exact else PASSES)

            def down(c, m, slot, tiles, start, stop, exact):
                for t in tiles:
                    if start and not (isinstance(c, int) and c == 0):
                        pe.wait_ge(down_scaled, TT * (c - 1) + t + 1)
                    mm = product(DOWN[t][:], lambda a, _: HT[a][:, slot, t * P:(t + 1) * P],
                                 lambda b, _: FW[b][:, m, 2, :], [0], start, stop,
                                 EXACT_MOVING if exact else PASSES)
                    if stop:
                        mm.then_inc(down_mm, 1)

            def step(c, m, slot, before, exact, split_weights=False, before_up=None, after_up=None):
                n = MT * c + m
                first, final = (isinstance(before[1], int) and before[1] == v for v in (0, MT - 1))
                if split_weights:
                    pe.wait_ge(fw_lo, 3 * m + 3)
                if isinstance(m, int) and m == 0:
                    pe.wait_ge(xt_lo, KT * (c + 1))
                pe.wait_ge(gate_silu, n)
                project_ffn(GATE, 0, c, m, exact).then_inc(gate_mm, 1)
                pe.wait_ge(ht_lo, n)
                down(*before, (0, 1), first, final, exact)
                if before_up:
                    before_up()
                pe.wait_ge(hidden_ok, n)
                project_ffn(UP, 1, c, m, exact).then_inc(up_mm, 1)
                if after_up:
                    after_up()
                down(*before, (2, 3), first, final, exact)

            def steps(c, lo, hi, exact, split_weights=False):
                with pe.Fori(lo // 2, hi // 2) as i:
                    for par in range(2):
                        step(c, 2 * i + par, par, (c, 2 * i + par - 1, 1 - par), exact, split_weights)

            def begin_chunk(c, exact, transposes=None):
                step(c - 1, MT - 1, 2, (c - 1, MT - 2, 1), exact, False, transposes)
                step(c, 0, 0, (c - 1, MT - 1, 2), exact)

            def transpose_rest():
                for k in range(2, KT):
                    transpose_x(1, k)

            def later_chunks(exact):
                begin_chunk(1, exact, transpose_rest)
                with pe.Fori(1, B - 1) as c:
                    step(c, 1, 1, (c, 0, 0), exact)
                    steps(c, 2, 6, exact)
                    for k in range(2):
                        transpose_x(c + 1, k)
                    steps(c, 6, 10, exact)
                    for k in range(2, KT):
                        transpose_x(c + 1, k)
                    begin_chunk(c + 1, exact)
                step(B - 1, 1, 1, (B - 1, 0, 0), exact)
                steps(B - 1, 2, 10, exact)
                step(B - 1, MT - 1, 2, (B - 1, MT - 2, 1), exact)

            def attention_begins(exact):
                project_head(QB, Q_SL, 0, q_mm)
                project_head(KB, K_SL, 0, k_mm)
                pe.wait_ge(ht_lo, MT * B)
                project_v(0)
                down(B - 1, MT - 1, 2, (0, 1), False, True, exact)
                project_v(1)
                down(B - 1, MT - 1, 2, (2, 3), False, True, exact)

            pe.wait_ge(ident_ok, 2)
            for k in range(KT):
                transpose_x(0, k)
            pe.wait_ge(fw_lo, 1)
            for k in range(KT):
                pe.wait_ge(xt_lo, k + 1)
                mm = project_ffn(GATE, 0, 0, 0, False, [k], k == 0, k == KT - 1)
            mm.then_inc(gate_mm, 1)
            pe.wait_ge(fw_lo, 2)
            project_ffn(UP, 1, 0, 0, False).then_inc(up_mm, 1)

            def check(m):
                pe.wait_ge(lo_summed, m)
                first = isinstance(m, int) and m == FIRST_CHECKED
                if first:
                    pe.wait_ge(lo_maxed, 1)
                nc.tensor.matmul(XB[0][0:1, 0:m + 1 if first else 1], ones[:],
                                 lo_sums[:, 0:m + 1] if first else lo_sums[:, ds(m, 1)],
                                 start=True, stop=True).then_inc(lo_mm, 1)

            step(0, 1, 1, (0, 0, 0), False, True,
                 after_up=lambda: check(FIRST_CHECKED))

            def checked_step(m, par):
                pe.wait_ge(lo_known, 2 * (m - 1))
                pe.sem_inc(branching, 1)
                exact = pe.value_load(exact_flag[:], min_val=0, max_val=1)
                with pe.If(exact):
                    step(0, m, par, (0, m - 1, 1 - par), True, True, before_up=lambda: check(m + 1))
                with pe.Else():
                    step(0, m, par, (0, m - 1, 1 - par), False, True, before_up=lambda: check(m + 1))

            with pe.Fori(1, (MT - 1) // 2) as i:
                for par in range(2):
                    checked_step(2 * i + par, par)

            def project_head(bank_, sl, n, signal):
                xo = ((n // HG) % B) * S
                product(bank_[:], lambda a, k: w_at(n, a, sl + k, (n % HG) * E, E),
                        lambda b, k: XT[b][:, k, ds(xo, S)], range(KT)).then_inc(signal, 1)

            def project_v(t):
                product(v_bank(t)[:], lambda a, k: XT[a][:, k, ds((t % (T // P)) * P, P)],
                        lambda b, k: w_at(t, b, V_SL + k), range(KT)).then_inc(v_mm, 1)

            def scores():
                for i, b_, col, _ in SCORE_TILES:
                    width = (i + 1) * P
                    mm = product(SC[b_][:, col:col + width], lambda a, _: Q[a][:, i * P:(i + 1) * P],
                                 lambda b, _: K[b][:, 0:width], [0])
                    if i != 2:
                        mm.then_inc(score_mm, 1)

            def weigh_v(u):
                def part(a, b, j, first=False, last=False):
                    return nc.tensor.matmul(ZB[:, j * P:], V[a][:, (u // HG) % 2, j, ds((u % HG) * E, E)],
                                            PT[b][:, (J_STEP + 1) * j:J_STEP * j + TT, :].rearrange("p i q -> p (i q)"),
                                            start=first, stop=last)
                pe.wait_ge(pt_ok[0], 16 * (u + 1))
                for j in range(TT):
                    part(0, 0, j, first=j == 0)
                    part(1, 0, j)
                pe.wait_ge(pt_ok[1], 16 * (u + 1))
                for j in range(TT):
                    mm = part(0, 1, j, last=j == TT - 1)
                mm.then_inc(z_mm, 1)

            def weigh_last_v():
                u = NU - 1
                pe.wait_ge(pt_ok[0], 16 * NU)
                pe.wait_ge(pt_ok[1], 16 * NU)
                for half in (0, 1):
                    keys = range(2 * (half + 1))
                    for j in keys:
                        i0 = max(j, 2 * half)
                        mm = product(LAST_Z[half][:, (i0 - 2 * half) * P:2 * P],
                                     lambda a, _: V[a][:, (u // HG) % 2, j, ds((u % HG) * E, E)],
                                     lambda b, _: PT[b][:, J_STEP * j + i0:J_STEP * j + 2 * half + 2, :]
                                     .rearrange("p i q -> p (i q)"), [0], j == 0, j == keys[-1])
                    mm.then_inc(z_mm, 1)

            def project_out(to, t, heads=range(HG), first=True, last=True):
                return product(to, lambda a, j: Z[a][:, (t // TT) % 2, j, ds((t % TT) * P, P)],
                               lambda b, j: w_at(t, b, O_SL + j), heads, first, last)

            def unit(u, v=True, out=True, more_w=True):
                if more_w:
                    pe.wait_ge(w_lo, u + 13)
                pe.wait_ge(q_lo, u + 1)
                project_head(QB, Q_SL, u + 1, q_mm)
                pe.wait_ge(k_lo, u + 1)
                project_head(KB, K_SL, u + 1, k_mm)
                if v:
                    pe.wait_ge(v_lo, u + 4)
                    project_v(u + 4)
                if out and not v:
                    pe.wait_ge(z_lo, 60)
                    project_out_tile(u - 4)
                pe.wait_ge(exp_ok, 2 * (u + 1))
                pe.wait_ge(q_lo, u + 2)
                pe.wait_ge(k_lo, u + 2)
                scores()
                if not (isinstance(u, int) and u == 0):
                    pe.wait_ge(z_lo, u)
                if out and v:
                    project_out_tile(u - 4)
                weigh_v(u)

            def project_out_tile(t):
                if isinstance(t, int) and t == 0:
                    pe.wait_ge(down_scaled, TT * B)
                else:
                    pe.wait_ge(out_added, t)
                project_out(OB[:], t).then_inc(out_mm, 1)

            pe.wait_ge(lo_known, 2 * (MT - FIRST_CHECKED))
            for k in range(2):
                transpose_x(1, k)
            exact = pe.value_load(exact_flag[:], min_val=0, max_val=1)
            with pe.If(exact):
                later_chunks(True)
                pe.wait_ge(w_lo, SLICES)
                attention_begins(True)
            with pe.Else():
                later_chunks(False)
                pe.wait_ge(w_lo, SLICES)
                attention_begins(False)
            pe.wait_ge(v_lo, 1)
            project_v(2)
            pe.wait_ge(v_lo, 2)
            pe.wait_ge(down_scaled, TT * (B - 1) + 2)
            scores()
            pe.wait_ge(v_lo, 3)
            project_v(3)
            pe.wait_ge(down_scaled, TT * B)
            unit(0, out=False)
            with pe.Fori(1, 4) as u:
                unit(u, out=False)
            unit(4)
            with pe.Fori(5, 48) as u:
                unit(u)
            pe.wait_ge(w_lo, B * SLICES)
            with pe.Fori(48, 60) as u:
                unit(u, more_w=False)
            pe.wait_ge(v_lo, NU)
            with pe.Fori(60, 63) as u:
                unit(u, v=False, more_w=False)
            project_out_tile(59)
            for heads in (range(2), [2]):
                if heads == [2]:
                    pe.wait_ge(z_lo, NU - 1)
                for t in range(TT):
                    if t == TT - 1 and heads != [2]:
                        pe.wait_ge(out_added, 60)
                    project_out(LAST[t][:], 60 + t, heads, first=heads != [2], last=False)
            pe.wait_ge(exp_ok, 2 * NU)
            weigh_last_v()
            for half in (0, 1):
                pe.wait_ge(z_lo, NU + half)
                for t in (2 * half, 2 * half + 1):
                    project_out(LAST[t][:], 60 + t, [HG - 1], first=False).then_inc(last_mm, 1)

        @block.scalar
        def _(act):
            def split_ffn(m, par):
                act.wait_ge(ffn_loaded[par], 16 * (m // 2 + 1))
                for w in range(3):
                    nc.scalar.activation(FW[0][:, m, w, :], ffn_in[:, par, w], ACT.Copy, scale=WS).then_inc(fw_hi, 1)

            def sum_lo(m):
                act.wait_ge(fw_lo, 3 * m + 3)
                if m > 0:
                    act.wait_ge(lo_summed, m - 1)
                nc.scalar.activation(lo_abs[:], FW[1][:, m].rearrange("p w n -> p (w n)"), ACT.Abs,
                                     accum_out=lo_sums[:, m:m + 1]).then_inc(lo_summed, 1)

            def split_attn(sl):
                act.wait_ge(w_loaded, 16 * (sl + 1))
                nc.scalar.activation(w_at(sl, 0, sl % SLICES), w_in[:, sl % 2], ACT.Copy, scale=WS).then_inc(w_hi, 1)

            def root(c):
                act.wait_ge(var_ok, c + 1)
                nc.scalar.activation(std[:], var_eps[:], ACT.Sqrt).then_inc(std_ok, 1)

            def split_x(c, k):
                act.wait_ge(xt_mm, KT * c + k + 1)
                nc.scalar.activation(XT[0][:, k, ds(c * S, S)], xt_bank(c, k)[:], ACT.Copy).then_inc(xt_hi, 1)

            def silu_down(c, tiles):
                for t in tiles:
                    act.wait_ge(down_scaled, TT * c + t + 1)
                    nc.scalar.activation(ffn_out[:, t], ffn_out[:, t], ACT.Silu).then_inc(down_silu, 1)

            def park(c):
                act.wait_ge(down_silu, TT * (c + 1))
                act.dma_start(parked_chunks[c], ffn_out).then_inc(park_done, 16)

            def step(c, m, slot, down_of=None, x_of=None):
                n = MT * c + m
                act.wait_ge(gate_mm, n + 1)
                nc.scalar.activation(silu_gate, GATE[:], ACT.Silu, scale=ffn_scales[:, ds(m, 1)]).then_inc(gate_silu, 1)
                if x_of is not None:
                    split_x(x_of, 2)
                    split_x(x_of, 3)
                if down_of is not None:
                    silu_down(down_of, (0, 1))
                act.wait_ge(hidden_ok, n + 1)
                nc.scalar.activation(HT[0][:, slot], hidden, ACT.Copy).then_inc(ht_hi, 1)
                if down_of is not None:
                    silu_down(down_of, (2, 3))
                    park(down_of)

            def step_and_slice(c, m, slot):
                step(c, m, slot)
                if c >= 2:
                    split_attn(m - 2 + 8 * (c - 2))

            def steps(c, lo, hi):
                with act.Fori(lo // 2, hi // 2) as i:
                    for par in range(2):
                        step_and_slice(c, 2 * i + par, par)

            def end_chunk(c):
                if c > 0:
                    split_x(c + 1, 2)
                    split_x(c + 1, 3)
                step(c, MT - 1, 2, x_of=1 if c == 0 else None)
                step(c + 1, 0, 0, down_of=c)

            root(0)
            act.wait_ge(ident_ok, 1)
            nc.scalar.activation(silu_gate[:, 0:1], ones[:], ACT.Silu)
            split_ffn(0, 0)
            for k in range(KT):
                split_x(0, k)
            split_ffn(1, 1)
            sum_lo(0)
            act.wait_ge(const_scaled, 3)
            for m in range(MT - 1):
                step(0, m, m % 2)
                for tile in SUMMED_BEFORE[m]:
                    sum_lo(tile)
                for tile in AHEAD[m]:
                    split_ffn(tile, tile % 2)
                for tile in SUMMED_BEHIND[m]:
                    sum_lo(tile)
                if m == 7:
                    root(1)
            split_x(1, 0)
            split_x(1, 1)
            end_chunk(0)
            for c in range(1, B):
                step(c, 1, 1)
                if c < B - 1:
                    step_and_slice(c, 2, 0)
                    root(c + 1)
                    step_and_slice(c, 3, 1)
                    steps(c, 4, 6)
                    split_x(c + 1, 0)
                    split_x(c + 1, 1)
                    steps(c, 6, 10)
                    end_chunk(c)
            steps(B - 1, 2, 10)
            step(B - 1, MT - 1, 2)

            def split_heads(n):
                act.wait_ge(q_mm, n + 1)
                nc.scalar.activation(Q[0][:], QB[:], ACT.Identity, bias=bias_of(0, n)).then_inc(q_hi, 1)
                act.wait_ge(k_mm, n + 1)
                nc.scalar.activation(K[0][:], KB[:], ACT.Identity, bias=bias_of(1, n)).then_inc(k_hi, 1)

            def split_v(t):
                act.wait_ge(v_mm, t + 1)
                nc.scalar.activation(V[0][:, (t // TT) % 2, t % TT, :], v_bank(t)[:], ACT.Copy).then_inc(v_hi, 1)

            def exps(n):
                for i, b_, col, at in SCORE_TILES:
                    width = (i + 1) * P
                    if i >= TT - 2:
                        act.wait_ge(negated, 2 * n + TT - i)
                    e = nc.scalar.activation(probs[:, at:at + width], SC[b_][:, col:col + width], ACT.Exp,
                                             bias=neg_max[:, i:i + 1], scale=SCORE_SCALE,
                                             accum_out=row_sum[:, i:i + 1])
                    if i in (TT - 1, 1):
                        e.then_inc(exp_ok, 1)

            def split_probs(n):
                if not (isinstance(n, int) and n == 0):
                    act.wait_ge(pt_ok[0], 16 * n)
                for i, _, _, at in SCORE_TILES:
                    if i >= TT - 2:
                        act.wait_ge(inverted, 2 * n + TT - i)
                    nc.scalar.activation(query_blocks(0, i), probs_by_block(i, at), ACT.Copy,
                                         scale=inv_sum[:, i:i + 1]).then_inc(p_hi, 1)

            def split_z(u):
                act.wait_ge(z_mm, u + 1)
                nc.scalar.activation(Z[0][:, (u // HG) % 2, u % HG, :], ZB[:], ACT.Identity,
                                     bias=bias_of(2, u)).then_inc(z_hi, 1)

            def unit(u, v=True, more_w=True):
                if not v:
                    split_z(u - 1)
                split_heads(u + 1)
                if v and not (isinstance(u, int) and u == 0):
                    split_z(u - 1)
                if v:
                    split_v(u + 4)
                if more_w:
                    split_attn(u + SLICES)
                exps(u + 1)
                split_probs(u + 1)

            split_heads(0)
            split_v(0)
            silu_down(B - 1, (0, 1))
            split_v(1)
            silu_down(B - 1, (2, 3))
            park(B - 1)
            split_v(2)
            exps(0)
            split_v(3)
            split_probs(0)
            unit(0)
            with act.Fori(1, 48) as u:
                unit(u)
            with act.Fori(48, 60) as u:
                unit(u, more_w=False)
            with act.Fori(60, 63) as u:
                unit(u, v=False, more_w=False)
            split_z(62)
            for half in (0, 1):
                act.wait_ge(z_mm, NU + half)
                nc.scalar.activation(last_z_part(0, half), LAST_Z[half][:, 0:2 * P], ACT.Identity,
                                     bias=bias_of(2, NU - 1)).then_inc(z_hi, 1)

        @block.vector
        def _(dve):
            def split_ffn(m, par, parts=range(3)):
                for w in parts:
                    dve.wait_ge(fw_hi, 3 * m + w + 1)
                    nc.vector.scalar_tensor_tensor(out=FW[1][:, m, w, :], in0=ffn_in[:, par, w], scalar=WS,
                                                   in1=FW[0][:, m, w, :], op0=ALU.mult,
                                                   op1=ALU.subtract).then_inc(fw_lo, 1)
                if m == DVE_LO:
                    dve.wait_ge(fw_lo, 3 * m + 3)
                    nc.vector.tensor_reduce(lo_sums[:, m:m + 1], FW[1][:, m].rearrange("p w n -> p (w n)"), AX_X,
                                            ALU.max, apply_absolute_value=True).then_inc(lo_maxed, 1)

            def split_attn(sl):
                dve.wait_ge(w_hi, sl + 1)
                nc.vector.scalar_tensor_tensor(out=w_at(sl, 1, sl % SLICES), in0=w_in[:, sl % 2], scalar=WS,
                                               in1=w_at(sl, 0, sl % SLICES), op0=ALU.mult,
                                               op1=ALU.subtract).then_inc(w_lo, 1)

            def token_stats(c, tiles):
                for t in tiles:
                    dve.wait_ge(x_loaded[t], 16 * (c + 1))
                    nc.vector.bn_stats(out=stats[:, t], in_=x_in[:, t]).then_inc(stats_ok, 1)

            def variances(c):
                for t in range(TT):
                    dve.wait_ge(stats_ok, TT * c + t + 1)
                    nc.vector.bn_aggr(out=moments[:, t], in_=stats[:, t]).then_inc(moments_ok, 1)
                dve.wait_ge(moments_ok, TT * (c + 1))
                nc.vector.tensor_scalar(var_eps[:], moments[:, :, 1], EPS, None, ALU.add).then_inc(var_ok, 1)

            def scale_x(c, tiles):
                if tiles[0] == 0:
                    invert_std(c)
                for t in tiles:
                    nc.vector.tensor_scalar(x_in[:, t], x_in[:, t], moments[:, t, 0:1], rstd[:, t:t + 1],
                                            ALU.subtract, ALU.mult).then_inc(xn_ok, 1)

            def invert_std(c):
                dve.wait_ge(std_ok, c + 1)
                nc.vector.reciprocal(rstd0[:], std[:]).then_inc(rstd_step, 1)
                dve.wait_ge(rstd_step, 4 * c + 1)
                nc.vector.tensor_tensor(newton_a[:], rstd0[:], rstd0[:], ALU.mult).then_inc(rstd_step, 1)
                dve.wait_ge(rstd_step, 4 * c + 2)
                nc.vector.scalar_tensor_tensor(out=newton_b[:], in0=newton_a[:], scalar=-0.5, in1=var_eps[:],
                                               op0=ALU.mult, op1=ALU.mult).then_inc(rstd_step, 1)
                dve.wait_ge(rstd_step, 4 * c + 3)
                nc.vector.scalar_tensor_tensor(out=rstd[:], in0=newton_b[:], scalar=1.5, in1=rstd0[:],
                                               op0=ALU.add, op1=ALU.mult).then_inc(rstd_step, 1)
                dve.wait_ge(rstd_step, 4 * c + 4)

            def split_x(c, k):
                dve.wait_ge(xt_hi, KT * c + k + 1)
                nc.vector.tensor_tensor(XT[1][:, k, ds(c * S, S)], xt_bank(c, k)[:], XT[0][:, k, ds(c * S, S)],
                                        ALU.subtract).then_inc(xt_lo, 1)

            def scale_down(c, tiles):
                for t in tiles:
                    dve.wait_ge(down_mm, TT * c + t + 1)
                    if t == 0 and not (isinstance(c, int) and c == 0):
                        dve.wait_ge(park_done, 16 * c)
                    nc.vector.tensor_tensor(ffn_out[:, t], DOWN[t][:], down_rows[:], ALU.mult).then_inc(down_scaled, 1)

            def step(c, m, slot, down_of=None, x_of=None):
                n = MT * c + m
                if down_of is not None:
                    scale_down(down_of, (0, 1))
                if x_of is not None:
                    split_x(x_of, 2)
                    split_x(x_of, 3)
                dve.wait_ge(gate_silu, n + 1)
                dve.wait_ge(up_mm, n + 1)
                nc.vector.scalar_tensor_tensor(out=hidden, in0=UP[:], scalar=ffn_scales[:, ds(MT + m, 1)],
                                               in1=silu_gate, op0=ALU.mult, op1=ALU.mult).then_inc(hidden_ok, 1)
                dve.wait_ge(ht_hi, n + 1)
                nc.vector.tensor_tensor(HT[1][:, slot], hidden, HT[0][:, slot], ALU.subtract).then_inc(ht_lo, 1)
                if down_of is not None:
                    scale_down(down_of, (2, 3))

            def step_and_slice(c, m, slot):
                step(c, m, slot)
                if c >= 2:
                    split_attn(m - 2 + 8 * (c - 2))

            def steps(c, lo, hi):
                with dve.Fori(lo // 2, hi // 2) as i:
                    for par in range(2):
                        step_and_slice(c, 2 * i + par, par)

            def end_chunk(c):
                if c > 0:
                    split_x(c + 1, 2)
                    split_x(c + 1, 3)
                step(c, MT - 1, 2, x_of=1 if c == 0 else None)
                step(c + 1, 0, 0, down_of=c)

            token_stats(0, range(TT))
            variances(0)
            scale_x(0, range(TT))
            split_ffn(0, 0, [0])
            for k in range(KT):
                split_x(0, k)
            split_ffn(0, 0, [1, 2])
            dve.wait_ge(const_scaled, 3)
            split_ffn(1, 1)

            def check(m):
                n = m - FIRST_CHECKED
                dve.wait_ge(lo_mm, n + 1)
                if n == 0:
                    nc.vector.tensor_reduce(lo_total[:], XB[0][0:1, 0:m + 1], AX_X, ALU.add).then_inc(lo_known, 1)
                else:
                    nc.vector.tensor_tensor(lo_total[:], XB[0][0:1, 0:1], lo_total[:], ALU.add).then_inc(lo_known, 1)
                dve.wait_ge(lo_known, 2 * n + 1)
                nc.vector.tensor_scalar(exact_flag[:], lo_total[:], 0.0, None, ALU.is_equal).then_inc(lo_known, 1)

            for m in range(MT - 1):
                if m > 0:
                    check(m + 1)
                step(0, m, m % 2)
                for tile in AHEAD[m]:
                    split_ffn(tile, tile % 2)
                if m in (5, 6):
                    token_stats(1, (0, 1) if m == 5 else (2, 3))
                if m == 6:
                    variances(1)
                if m == 8:
                    scale_x(1, range(TT))
            split_x(1, 0)
            split_x(1, 1)
            end_chunk(0)
            for c in range(1, B):
                step(c, 1, 1)
                if c < B - 1:
                    token_stats(c + 1, range(TT))
                    variances(c + 1)
                    step_and_slice(c, 2, 0)
                    step_and_slice(c, 3, 1)
                    scale_x(c + 1, (0, 1))
                    step_and_slice(c, 4, 0)
                    scale_x(c + 1, (2, 3))
                    step_and_slice(c, 5, 1)
                    split_x(c + 1, 0)
                    split_x(c + 1, 1)
                    steps(c, 6, 10)
                    end_chunk(c)
            steps(B - 1, 2, 10)
            step(B - 1, MT - 1, 2)

            def split_heads(n):
                dve.wait_ge(q_hi, n + 1)
                nc.vector.scalar_tensor_tensor(out=Q[1][:], in0=QB[:], scalar=bias_of(0, n), in1=Q[0][:],
                                               op0=ALU.add, op1=ALU.subtract).then_inc(q_lo, 1)
                dve.wait_ge(k_hi, n + 1)
                nc.vector.scalar_tensor_tensor(out=K[1][:], in0=KB[:], scalar=bias_of(1, n), in1=K[0][:],
                                               op0=ALU.add, op1=ALU.subtract).then_inc(k_lo, 1)

            def split_v(t):
                dve.wait_ge(v_hi, t + 1)
                at = (t // TT) % 2
                nc.vector.tensor_tensor(V[1][:, at, t % TT, :], v_bank(t)[:], V[0][:, at, t % TT, :],
                                        ALU.subtract).then_inc(v_lo, 1)

            def maxima(n):
                for b_, col, blocks in DIAGONALS:
                    dve.wait_ge(score_mm, 3 * n + b_ + 1)
                    nc.vector.tensor_tensor(SC[b_][:, col:col + blocks * P], SC[b_][:, col:col + blocks * P],
                                            mask[:, 0:blocks, :].rearrange("p b k -> p (b k)"),
                                            ALU.add).then_inc(masked, 1)
                for g, (i, b_, col, _) in enumerate(SCORE_TILES):
                    if g < 3:
                        dve.wait_ge(masked, 3 * n + g + 1)
                    nc.vector.reduce_max(row_max[:, i:i + 1], SC[b_][:, col:col + (i + 1) * P], AX_X).then_inc(maxed, 1)
                    if g in (1, TT - 1):
                        dve.wait_ge(maxed, TT * n + (1 if g == 1 else TT))
                        cols_ = slice(TT - 1, TT) if g == 1 else slice(0, TT - 1)
                        nc.vector.tensor_scalar(neg_max[:, cols_], row_max[:, cols_], -SCORE_SCALE, None,
                                                ALU.mult).then_inc(negated, 1)

            def invert_sums(n):
                for half, cols_ in enumerate((slice(TT - 1, TT), slice(0, TT - 1))):
                    dve.wait_ge(exp_ok, 2 * n + half + 1)
                    nc.vector.reciprocal(inv_sum[:, cols_], row_sum[:, cols_]).then_inc(inverted, 1)

            def split_probs(n):
                if not (isinstance(n, int) and n == 0):
                    dve.wait_ge(pt_ok[1], 16 * n)
                for g, (i, _, _, at) in enumerate(SCORE_TILES):
                    dve.wait_ge(p_hi, TT * n + g + 1)
                    nc.vector.scalar_tensor_tensor(out=query_blocks(1, i), in0=probs_by_block(i, at),
                                                   scalar=inv_sum[:, i:i + 1], in1=query_blocks(0, i),
                                                   op0=ALU.mult, op1=ALU.subtract).then_inc(p_lo, 1)

            def split_z(u):
                dve.wait_ge(z_hi, u + 1)
                at = (u // HG) % 2
                nc.vector.scalar_tensor_tensor(out=Z[1][:, at, u % HG, :], in0=ZB[:], scalar=bias_of(2, u),
                                               in1=Z[0][:, at, u % HG, :], op0=ALU.add,
                                               op1=ALU.subtract).then_inc(z_lo, 1)

            def add_out(t):
                dve.wait_ge(out_mm, t + 1)
                o = t % (T // P)
                nc.vector.scalar_tensor_tensor(out=acc[:, o], in0=OB[:], scalar=WS ** -2, in1=acc[:, o],
                                               op0=ALU.mult, op1=ALU.add).then_inc(out_added, 1)

            def unit(u, v=True, out=True, more_w=True):
                if not v:
                    split_z(u - 1)
                split_heads(u + 1)
                if v and not (isinstance(u, int) and u == 0):
                    split_z(u - 1)
                if v:
                    split_v(u + 4)
                if more_w:
                    split_attn(u + SLICES)
                if out and not v:
                    add_out(u - 4)
                maxima(u + 1)
                invert_sums(u + 1)
                if out and v:
                    add_out(u - 4)
                split_probs(u + 1)

            split_heads(0)
            split_v(0)
            scale_down(B - 1, (0, 1))
            split_v(1)
            scale_down(B - 1, (2, 3))
            split_v(2)
            dve.wait_ge(ident_ok, 2)
            maxima(0)
            split_v(3)
            invert_sums(0)
            split_probs(0)
            unit(0, out=False)
            with dve.Fori(1, 4) as u:
                unit(u, out=False)
            dve.wait_ge(acc_ready, T // P)
            with dve.Fori(4, 48) as u:
                unit(u)
            with dve.Fori(48, 60) as u:
                unit(u, more_w=False)
            with dve.Fori(60, 63) as u:
                unit(u, v=False, more_w=False)
            add_out(59)
            split_z(62)
            for half in (0, 1):
                dve.wait_ge(z_hi, NU + half)
                nc.vector.scalar_tensor_tensor(out=last_z_part(1, half), in0=LAST_Z[half][:, 0:2 * P],
                                               scalar=bias_of(2, NU - 1), in1=last_z_part(0, half),
                                               op0=ALU.add, op1=ALU.subtract).then_inc(z_lo, 1)
            for t in range(TT):
                if t == 0:
                    dve.wait_ge(base_ok, TT)
                dve.wait_ge(last_mm, t + 1)
                nc.vector.scalar_tensor_tensor(out=silu_last[:, t], in0=LAST[t][:], scalar=WS ** -2,
                                               in1=silu_last[:, t], op0=ALU.mult, op1=ALU.mult).then_inc(last_mul, 1)
            for t in (2, 3):
                dve.wait_ge(last_mul, t + 1)
                nc.vector.tensor_tensor(silu_last[:, t], silu_last[:, t], acc[:, TAIL + t],
                                        ALU.add).then_inc(last_sum, 1)


def kernel(L0_attn_x, L0_attn_W_Q, L0_attn_W_K, L0_attn_W_V, L0_attn_W_O, L0_attn_b_Q, L0_attn_b_K, L0_attn_b_V,
           L0_attn_b_O, L0_ffn_gate_w, L0_ffn_up_w, L0_ffn_down_w, L0_ffn_gate_s, L0_ffn_up_s, L0_ffn_down_s):
    import numpy as np
    import concourse.bacc as bacc
    from concourse.bass_utils import run_bass_kernel_spmd

    x = np.ascontiguousarray(L0_attn_x).reshape(T, D)

    def up_like(w):
        return np.asarray(w).reshape(MT, P, KT, P).transpose(0, 3, 2, 1).reshape(MT, P, 1, 512)
    down = np.asarray(L0_ffn_down_w).T.reshape(MT, P, 1, D)
    ffn_w = np.ascontiguousarray(np.concatenate([up_like(L0_ffn_gate_w), up_like(L0_ffn_up_w), down], axis=2))

    def by_feature(w):
        return np.asarray(w).reshape(H // HG, HG, KT, P, E).transpose(0, 2, 3, 1, 4).reshape(H // HG, KT, P, HG * E)
    w_o = np.asarray(L0_attn_W_O).reshape(H // HG, HG, E, D)
    attn_w = np.ascontiguousarray(np.concatenate(
        [by_feature(L0_attn_W_V), by_feature(L0_attn_W_Q), by_feature(L0_attn_W_K), w_o], axis=1)).reshape(-1, P, 512)

    cols = np.ascontiguousarray(np.concatenate(
        [np.asarray(b).T for b in (L0_attn_b_Q, L0_attn_b_K, L0_attn_b_V)]
        + [np.asarray(v).reshape(MT, P).T for v in (L0_ffn_gate_s, L0_ffn_up_s)], axis=1))

    arrays = {"x": x, "ffn_w": ffn_w, "attn_w": attn_w, "cols": cols,
              "b_o": np.ascontiguousarray(L0_attn_b_O), "down_s": np.ascontiguousarray(L0_ffn_down_s)}
    nc = bacc.Bacc("TRN2", target_bir_lowering=False, num_devices=1)
    args = [nc.dram_tensor(f"{n}_dram", a.shape, F32, kind="ExternalInput").ap() for n, a in arrays.items()]
    out = nc.dram_tensor("out_dram", (T, D), F32, kind="ExternalOutput").ap()
    build(nc, *args, out)
    r = run_bass_kernel_spmd(nc, [{f"{n}_dram": a for n, a in arrays.items()}], core_ids=[0])
    return r.results[0]["out_dram"].reshape(B, S, D)
```
